# Optimizing a Trainium2 kernel written in Bass

```python
import numpy as np
import jax
import jax.numpy as jnp

def _softmax(x, axis=-1):
    return jax.nn.softmax(x, axis=axis)

def _gelu(x):
    return jax.nn.gelu(x, approximate=True)

def _silu(x):
    return jax.nn.silu(x)

def _sigmoid(x):
    return jax.nn.sigmoid(x)

def _layernorm(x, axis=-1, eps=1e-05):
    m = jnp.mean(x, axis=axis, keepdims=True)
    v = jnp.var(x, axis=axis, keepdims=True)
    return (x - m) / jnp.sqrt(v + eps)

def _scatter_add(tgt, idx, src, axis=0):
    return tgt.at[idx].add(src)

def _segment_sum(src, seg, n):
    return jax.ops.segment_sum(src, seg, n)
kernel_name = 'mk_cond_seq_d2_seqx_r2_309a82'

def setup_inputs(seed: int=0):
    np.random.seed(seed)
    _w = jnp.asarray

    def _rec_inputs():
        import jax
        import jax.numpy as jnp
        _rk = jax.random.key(seed)
        x = -0.0002928 + 1 * jax.random.normal(jax.random.fold_in(_rk, 1), (128, 128, 512), jnp.float32)
        _lenS = 128 - jax.random.randint(jax.random.fold_in(_rk, 7), (128,), 0, max(1, 128 // 4) + 1, jnp.int32)
        _lenS2 = 128 - jax.random.randint(jax.random.fold_in(_rk, 8), (128,), 0, max(1, 128 // 4) + 1, jnp.int32)
        itok_B_0_7 = jax.random.randint(jax.random.fold_in(_rk, 11), (128,), 0, 8, jnp.int32)
        condB_theta = jax.random.uniform(jax.random.fold_in(_rk, 12), (128,), jnp.float32, 0.0, 0.983423)
        condB_phi = jax.random.uniform(jax.random.fold_in(_rk, 13), (128,), jnp.float32, 0.0, 0.961312)
        return (x, itok_B_0_7, condB_theta, condB_phi)
    x, itok_B_0_7, condB_theta, condB_phi = _rec_inputs()

    def _L0_cond_setup():
        import jax, jax.numpy as jnp
        import numpy as np
        E, H, I = (8, 512, 2048)
        B, S = (4, 512)
        LN_EPS = 1e-12
        key = jax.random.key(seed)
        ks = jax.random.split(key, 8)
        x = jax.random.normal(ks[0], (B, S, H), dtype=jnp.float32)
        expert_idx = jax.random.randint(ks[1], (B,), 0, E, dtype=jnp.int64)
        Wi = jax.random.normal(ks[2], (E, H, I), dtype=jnp.float32) * 0.02
        bi = jnp.zeros((E, I), dtype=jnp.float32)
        Wo = jax.random.normal(ks[3], (E, I, H), dtype=jnp.float32) * 0.02
        bo = jnp.zeros((E, H), dtype=jnp.float32)
        gamma = jnp.ones((E, H), dtype=jnp.float32)
        beta = jnp.zeros((E, H), dtype=jnp.float32)
        return {'input_tensor': x, 'expert_idx': expert_idx, 'Wi': Wi, 'bi': bi, 'Wo': Wo, 'bo': bo, 'gamma': gamma, 'beta': beta}
    _L0_cond_all = _L0_cond_setup()
    _L0_cond_in = {k: v for k, v in _L0_cond_all.items() if k in ('Wi', 'bi', 'Wo', 'bo', 'gamma', 'beta')}
    del _L0_cond_all

    def _L1_cond_setup():
        import jax, jax.numpy as jnp
        import numpy as np
        key = jax.random.key(seed)
        k1, k2, k3 = jax.random.split(key, 3)
        B, N, D = (16, 2048, 512)
        embeddings = jax.random.normal(k1, (B, N, D), dtype=jnp.float32)
        theta = jax.random.uniform(k2, (B,), dtype=jnp.float32)
        phi = jax.random.uniform(k3, (B,), dtype=jnp.float32)
        return {'embeddings': embeddings, 'theta': theta, 'phi': phi}
    _L1_cond_all = _L1_cond_setup()
    _L1_cond_in = {k: v for k, v in _L1_cond_all.items() if k in ()}
    del _L1_cond_all
    return {'x': x, 'itok_B_0_7': itok_B_0_7, 'condB_theta': condB_theta, 'condB_phi': condB_phi, 'L0_cond_Wi': _L0_cond_in['Wi'], 'L0_cond_bi': _L0_cond_in['bi'], 'L0_cond_Wo': _L0_cond_in['Wo'], 'L0_cond_bo': _L0_cond_in['bo'], 'L0_cond_gamma': _L0_cond_in['gamma'], 'L0_cond_beta': _L0_cond_in['beta']}

def reference(x, itok_B_0_7, condB_theta, condB_phi, L0_cond_Wi, L0_cond_bi, L0_cond_Wo, L0_cond_bo, L0_cond_gamma, L0_cond_beta):
    import jax
    import jax.numpy as jnp

    def _L0_cond_ref(input_tensor, expert_idx, Wi, bi, Wo, bo, gamma, beta):
        import jax, jax.numpy as jnp
        import numpy as np
        E, H, I = (8, 512, 2048)
        B, S = (4, 512)
        LN_EPS = 1e-12
        Wi_b = Wi[expert_idx]
        bi_b = bi[expert_idx]
        Wo_b = Wo[expert_idx]
        bo_b = bo[expert_idx]
        g_b = gamma[expert_idx]
        be_b = beta[expert_idx]
        h = jax.nn.gelu(jnp.einsum('bsh,bhi->bsi', input_tensor, Wi_b) + bi_b[:, None, :], approximate=False)
        o = jnp.einsum('bsi,bih->bsh', h, Wo_b) + bo_b[:, None, :]
        r = o + input_tensor
        mu = jnp.mean(r, axis=-1, keepdims=True)
        var = jnp.mean(jnp.square(r - mu), axis=-1, keepdims=True)
        y = (r - mu) * jax.lax.rsqrt(var + LN_EPS)
        return y * g_b[:, None, :] + be_b[:, None, :]

    def _L1_cond_ref(embeddings, theta, phi):
        import jax, jax.numpy as jnp
        import numpy as np
        B, N, D = embeddings.shape
        e = embeddings.reshape(B, N, D // 4, 4)
        ct = jnp.cos(theta)[:, None, None]
        st = jnp.sin(theta)[:, None, None]
        cp = jnp.cos(phi)[:, None, None]
        sp = jnp.sin(phi)[:, None, None]
        x0, x1, x2, x3 = (e[..., 0], e[..., 1], e[..., 2], e[..., 3])
        out = jnp.stack([x0 * ct + x1 * st, -x0 * st + x1 * ct, x2 * cp + x3 * sp, -x2 * sp + x3 * cp], axis=-1)
        return out.reshape(B, N, D)
    x = _L0_cond_ref(x, itok_B_0_7, L0_cond_Wi, L0_cond_bi, L0_cond_Wo, L0_cond_bo, L0_cond_gamma, L0_cond_beta)
    x = _L1_cond_ref(x, condB_theta, condB_phi)
    return x

_drawn_inputs = setup_inputs


def setup_inputs(seed=0):
    import zlib

    import numpy as np

    out = dict(_drawn_inputs(seed))
    spreads = {'L0_cond_bi': (0.0, 0.1),
     'L0_cond_bo': (0.0, 0.1),
     'L0_cond_gamma': (1.0, 0.2),
     'L0_cond_beta': (0.0, 0.1)}
    factors = {}
    for name, (base, spread) in spreads.items():
        noise = np.random.default_rng([zlib.crc32(name.encode()), seed]).standard_normal(out[name].shape)
        drawn = base * np.exp(spread * noise) if base else spread * noise
        out[name] = jnp.asarray(drawn.astype(out[name].dtype))
    for name, factor in factors.items():
        out[name] = (out[name] * factor).astype(out[name].dtype)
    return out
```

```python
import concourse.bass as bass
from concourse import mybir
from contextlib import ExitStack

F32 = mybir.dt.float32
F16 = mybir.dt.float16
I32 = mybir.dt.int32
ALU = mybir.AluOpType
ACT = mybir.ActivationFunctionType
AX = mybir.AxisListType
ADD_LANES = bass.bass_isa.ReduceOp.add

P = 128
BANK = 512
LN_EPS = 1e-12
EXP1 = 1 << 23
EXP2 = 1 << 24
SCALE, INVERSE, BOUND = 204, 50, 65
SCALE_F, INVERSE_F = 268, -14
TWO_PI_PARTS = (6.28125, 0.0019350051879882812, 3.0199159819567e-07)
TO_INTEGER = 1.5 * 2.0 ** 23
BELOW_PI = 3.1415925


class Steps:

    def __init__(self, engine, sem):
        self.engine, self.sem, self.n = engine, sem, 0

    def step(self, ins):
        ins.then_inc(self.sem, 1)
        self.n += 1
        self.engine.wait_ge(self.sem, self.n)

    def clear(self):
        self.engine.sem_clear(self.sem)
        self.n = 0


def expert_mlp_rotate_kernel(nc, x, itok, theta, phi, Wi, bi, Wo, bo, gamma, beta, out):
    S, T, H = x.shape
    E, _, I = Wi.shape
    KH, KI = H // P, I // P
    NB = I // BANK
    GC = KI // NB
    Q = 4
    QN = H * I // P // Q
    XB = 4
    assert T == P and S == P and H == BANK and E % 2 == 0 and NB == Q == KH

    ctx = ExitStack()
    with ctx:
        def sb(name, shape, dt=F32):
            return ctx.enter_context(nc.sbuf_tensor(name, shape, dt))

        def pb(name, shape, dt=F32):
            return ctx.enter_context(nc.psum_tensor(name, shape, dt))

        def sem(name):
            return ctx.enter_context(nc.semaphore(name))

        wi16 = sb("wi16", [P, 2, 2, KH, I], F16)
        wo16 = sb("wo16", [P, 2, 2, KI, H], F16)
        staged = sb("staged", [P, 2, QN])
        bi_all = sb("bi_all", [P, 2, I])
        bgb_all = sb("bgb_all", [P, 2, 3, H])
        hid = sb("hid", [P, I])
        hT16 = sb("hT16", [P, 2, 2, GC, P], F16)
        xbuf = sb("xbuf", [P, XB, H])
        xs = sb("xs", [P, H])
        xT16 = sb("xT16", [P, 2, KH, P], F16)
        y = sb("y", [P, H])
        turned = sb("turned", [P, H])
        rot = sb("rot", [P, S, 8])
        ident = sb("ident", [P, P])
        tab = sb("tab", [1, 3 * S + 2 * E + 1], I32)
        BATCH, RANK, BUF, EXPERT, BEFORE = 0, S, 2 * S, 3 * S, 3 * S + E
        tok = sb("tok", [P, 6])
        SS, SX, SH, ZS, TM, TB = (tok[:, j:j + 1] for j in range(6))
        inv = sb("inv", [P, XB, 2])
        ISX, ISH = range(2)
        ex = sb("ex", [P, 2, 4])
        IWI, AWI, NBI, IWO = range(4)
        wscale = sb("wscale", [P, 2])
        ln = sb("ln", [P, 16])
        consts = sb("consts", [P, 6], I32)
        pool_s = sb("pool_s", [P, 4])
        boot_ss = sb("boot_ss", [P, 2 * Q + 3])

        z_ps = pb("z_ps", [P, NB, BANK])
        hT_ps = pb("hT_ps", [P, 2, BANK])
        xT_ps = pb("xT_ps", [P, BANK])
        o_ps = pb("o_ps", [P, BANK])

        keys_i = hid[:, 0:129].bitcast(I32)
        iota_i = hid[:, 132:261].bitcast(I32)
        keys_e = hid[:, 264:393]
        keys_k = hid[:, 396:525]
        iota_f = hid[:, 528:657]
        less = hid[:, 660:788]
        onehot = hid[:, 792:920]
        onehot_r = hid[:, 924:924 + E]
        after_r = hid[:, 940:940 + E + 1]
        ones = hid[:, 960:961]
        cols = hid[:, 964:980]
        angle = hid[:, 980:1010]
        spread = hid[:, 1024:1024 + 4 * P]

        s_idx = sem("s_idx")
        s_iota = sem("s_iota")
        s_ident = sem("s_ident")
        s_pool = sem("s_pool")
        s_dve = sem("s_dve")
        s_act = sem("s_act")
        s_ang = sem("s_ang")
        s_sin = sem("s_sin")
        s_less = sem("s_less")
        s_rankp = sem("s_rankp")
        s_onehot = sem("s_onehot")
        s_tabp = sem("s_tabp")
        s_tables = sem("s_tables")
        s_braw = [sem(f"s_braw{i}") for i in range(2 * Q)]
        s_bsq = sem("s_bsq")
        s_bsum = sem("s_bsum")
        s_bscale = sem("s_bscale")
        s_bhi = sem("s_bhi")
        s_bias = [sem(f"s_bias{i}") for i in range(2)]
        s_stage = [sem(f"s_stage{i}") for i in range(2)]
        s_unstage = [sem(f"s_unstage{i}") for i in range(2)]
        s_wi = sem("s_wi")
        s_wo = sem("s_wo")
        s_x = sem("s_x")
        s_y = sem("s_y")
        s_sq = sem("s_sq")
        s_sx = sem("s_sx")
        s_xs = sem("s_xs")
        s_xT = sem("s_xT")
        s_xhi = sem("s_xhi")
        s_xlo = sem("s_xlo")
        s_g1 = sem("s_g1")
        s_z = sem("s_z")
        s_gelu = sem("s_gelu")
        s_hs = sem("s_hs")
        s_hT = sem("s_hT")
        s_hhi = sem("s_hhi")
        s_hlo = sem("s_hlo")
        s_g2 = sem("s_g2")
        s_res = sem("s_res")
        s_done = sem("s_done")

        block = ctx.enter_context(nc.Block())

        def slot_value(engine, table, s, top):
            return engine.value_load(tab[0:1, bass.ds(s + table, 1)], min_val=0, max_val=top)

        def pipeline(engine, iteration):
            iteration(-1)
            iteration(0)
            iteration(1)
            with engine.Fori(2, S - 2) as s:
                iteration(s, True)
            for s in range(S - 2, S + 2):
                iteration(s)

        def there(s, d, inner):
            return inner or 0 <= s + d < S

        @block.sync
        def _(sp):
            sp.dma_start(keys_i[:, 0:S], itok.partition_broadcast(P)).then_inc(s_idx, 16)
            sp.dma_start(keys_i[:, S:S + 1], itok.rearrange("(p o) -> p o", o=1)).then_inc(s_idx, 16)
            sp.dma_start(angle[:, 0:1], theta.rearrange("(p o) -> p o", o=1)).then_inc(s_idx, 16)
            sp.dma_start(angle[:, 1:2], phi.rearrange("(p o) -> p o", o=1)).then_inc(s_idx, 16)

            def weight_quarter(m, e, q):
                if m == 0:
                    return Wi[bass.ds(e, 1), q * P:(q + 1) * P, :].rearrange("e p n -> p (e n)")
                rows = slice(q * GC * P, (q + 1) * GC * P)
                return Wo[bass.ds(e, 1), rows, :].rearrange("e (c p) n -> p (e c) n", p=P)

            def quarter_view(region, m):
                return region if m == 0 else region.rearrange("p (c n) -> p c n", n=H)

            def load_biases(e, b):
                sp.dma_start(bi_all[:, b, :], bi[bass.ds(e, 1), :].broadcast_to([P, I])).then_inc(s_bias[b], 16)
                for j, v in enumerate((bo, gamma, beta)):
                    sp.dma_start(bgb_all[:, b, j, :], v[bass.ds(e, 1), :].broadcast_to([P, H])).then_inc(s_bias[b], 16)

            sp.wait_ge(s_tables, 1)
            e0 = slot_value(sp, EXPERT, 0, E - 1)
            for m, w in enumerate((wi16, wo16)):
                raw = w[:, 1].rearrange("p a k n -> p (a k n)").bitcast(F32)
                for q in range(Q):
                    sp.dma_start(quarter_view(raw[:, q * QN:(q + 1) * QN], m),
                                 weight_quarter(m, e0, q)).then_inc(s_braw[m * Q + q], 16)
                if m == 0:
                    load_biases(e0, 0)

            def rank(r, b, nth):
                if not (isinstance(r, int) and r == 1):
                    sp.wait_ge(s_done, slot_value(sp, BEFORE, r - 1, S + 1))
                e = slot_value(sp, EXPERT, r, E - 1)
                load_biases(e, b)
                j = 0
                for m in range(2):
                    for again in range(2):
                        for q in range(Q):
                            used = (r - 1) * (2 * Q) + j // 2
                            if not isinstance(used, int) or used > 0:
                                sp.wait_ge(s_unstage[j % 2], used)
                            sp.dma_start(quarter_view(staged[:, j % 2, :], m),
                                         weight_quarter(m, e, q)).then_inc(s_stage[j % 2], 16)
                            j += 1

            rank(1, 1, 0)
            with sp.Fori(1, E // 2) as i:
                rank(i * 2, 0, i)
                rank(i * 2 + 1, 1, i)

        @block.gpsimd
        def _(pool):
            g = nc.gpsimd
            chain = Steps(pool, s_pool)
            g.iota(iota_i[:, 0:S], [[1, S]], base=0, channel_multiplier=0)
            g.iota(iota_i[:, S:S + 1], [[1, 1]], base=0, channel_multiplier=1)
            for j, c in enumerate((EXP2, EXP1, SCALE * EXP1, INVERSE * EXP1, (INVERSE + 30) * EXP1,
                                   BOUND * EXP1)):
                last = g.memset(consts[:, j:j + 1], c)
            last.then_inc(s_iota, 1)
            chain.step(g.memset(ident[:], 0.0))
            g.affine_select(out=ident[:], in_=ident[:], compare_op=ALU.not_equal, fill=1.0, base=0,
                            pattern=[[-1, P]], channel_multiplier=1).then_inc(s_ident, 1)

            def scale_of(ss, scale_out, outs, chain):
                c = consts
                chain.step(g.tensor_tensor(pool_s[:, 1:2].bitcast(I32), ss.bitcast(I32), c[:, 0:1], ALU.divide))
                chain.step(g.tensor_tensor(pool_s[:, 2:3].bitcast(I32), pool_s[:, 1:2].bitcast(I32), c[:, 1:2], ALU.mult))
                t = pool_s[:, 2:3].bitcast(I32)
                if scale_out is not None:
                    chain.step(g.tensor_tensor(scale_out.bitcast(I32), c[:, 2:3], t, ALU.subtract))
                for o, j in outs:
                    chain.step(g.tensor_tensor(o.bitcast(I32), t, c[:, j:j + 1], ALU.add))

            def scales(what, ss, b, chain):
                col = lambda k: ex[:, b, k:k + 1]
                if what == "wi":
                    scale_of(ss, wscale[:, 0:1], [(col(IWI), 3), (col(AWI), 4)], chain)
                elif what == "wo":
                    scale_of(ss, wscale[:, 1:2], [(col(IWO), 3)], chain)
                else:
                    scale_of(ss, None, [(col(NBI), 5)], chain)

            for n, what in enumerate(("wi", "bi", "wo")):
                pool.wait_ge(s_bsum, n + 1)
                ss = boot_ss[:, 2 * Q + n:2 * Q + n + 1]
                if what != "bi":
                    chain.step(g.partition_all_reduce(pool_s[:, 0:1], ss, P, ADD_LANES))
                    ss = pool_s[:, 0:1]
                scales(what, ss, 0, chain)
                g.engine_nop().then_inc(s_bscale, 1)

            PIECE = 1024
            def rank(r, b, nth):
                chain.clear()
                boot = isinstance(r, int) and r == 1
                before = None if boot else slot_value(pool, BEFORE, r - 1, S + 1)

                def quarter(j):
                    pool.wait_ge(s_stage[j % 2], 16)
                    pool.sem_clear(s_stage[j % 2])
                    return staged[:, j % 2, :]

                def fold(acc):
                    w = QN // 2
                    while w:
                        chain.step(g.tensor_tensor(acc[:, 0:w], acc[:, 0:w], acc[:, w:2 * w], ALU.add))
                        w //= 2
                    return acc[:, 0:1]

                j = 0
                for m, w in enumerate((wi16, wo16)):
                    hi = w[:, b, 0].rearrange("p k n -> p (k n)")
                    lo = w[:, b, 1].rearrange("p k n -> p (k n)")
                    room = lo.bitcast(F32)
                    acc, sq = room[:, 0:QN], room[:, QN:2 * QN]
                    for q in range(Q):
                        raw = quarter(j)
                        if j == 0 and boot:
                            pool.wait_ge(s_wo, 1)
                        elif j == 0:
                            pool.wait_ge(s_done, before)
                        for at in range(0, QN, PIECE):
                            p = slice(at, at + PIECE)
                            to = (acc if q == 0 else sq)[:, p]
                            ins = g.tensor_tensor(to, raw[:, p], raw[:, p], ALU.mult)
                            chain.step(ins)
                            if q:
                                chain.step(g.tensor_tensor(acc[:, p], acc[:, p], sq[:, p], ALU.add))
                        g.engine_nop().then_inc(s_unstage[j % 2], 1)
                        j += 1
                    fold(acc)
                    chain.step(g.partition_all_reduce(pool_s[:, 0:1], acc[:, 0:1], P, ADD_LANES))
                    scales(("wi", "wo")[m], pool_s[:, 0:1], b, chain)
                    if m == 0:
                        pool.wait_ge(s_bias[b], nth * 64 + 64)
                        chain.step(g.tensor_tensor(acc, bi_all[:, b, :], bi_all[:, b, :], ALU.mult))
                        fold(acc)
                        scales("bi", acc[:, 0:1], b, chain)
                    for q in range(Q):
                        raw = quarter(j)
                        for at in range(0, QN, PIECE):
                            p, o = slice(at, at + PIECE), slice(q * QN + at, q * QN + at + PIECE)
                            s = wscale[:, m:m + 1]
                            chain.step(g.tensor_scalar(hi[:, o], raw[:, p], s, 1.0, ALU.mult, ALU.mult))
                            chain.step(g.tensor_scalar(raw[:, p], raw[:, p], s, 1.0, ALU.mult, ALU.mult))
                            chain.step(g.tensor_tensor(lo[:, o], raw[:, p], hi[:, o], ALU.subtract))
                        g.engine_nop().then_inc(s_unstage[j % 2], 1)
                        j += 1
                    g.engine_nop().then_inc((s_wi, s_wo)[m], 1)

            rank(1, 1, 0)
            with pool.Fori(1, E // 2) as i:
                rank(i * 2, 0, i)
                rank(i * 2 + 1, 1, i)

        @block.scalar
        def _(act):
            a = nc.scalar
            chain = Steps(act, s_act)
            act.wait_ge(s_ang, 1)
            a.activation(angle[:, 20:24], angle[:, 16:20], ACT.Sin).then_inc(s_sin, 1)
            act.wait_ge(s_tables, 1)

            def load_x(s, b):
                act.dma_start(xbuf[:, bass.ds(s % XB, 1), :].rearrange("p a n -> p (a n)"),
                              x[bass.ds(b, 1), :, :].rearrange("a t n -> t (a n)")).then_inc(s_x, 16)

            def iteration(s, inner=False):
                if there(s, 2, inner):
                    b = slot_value(act, BATCH, s + 2, S - 1)
                if there(s, 1, inner):
                    act.wait_ge(s_x, (s + 2) * 16)
                    if inner or s >= 0:
                        act.wait_ge(s_xT, s + 1)
                if there(s, 2, inner):
                    if inner or s >= 2:
                        act.wait_ge(s_res, s - 1)
                    load_x(s + 2, b)
                if there(s, 1, inner):
                    xv = xbuf[:, bass.ds((s + 1) % XB, 1), :].rearrange("p a n -> p (a n)")
                    a.activation(xs[:], xv, ACT.Square, accum_out=SS).then_inc(s_sq, 1)
                    act.wait_ge(s_sx, 1)
                    act.sem_clear(s_sx)
                    a.activation(xs[:], xv, ACT.Copy, scale=SX).then_inc(s_xs, 1)

                def hi_group(n):
                    G = (s - 1) * NB + n
                    act.wait_ge(s_hT, G + 1)
                    if inner or G >= 2:
                        act.wait_ge(s_g2, G - 1)
                    a.activation(hT16[:, n % 2, 0].rearrange("p c t -> p (c t)"), hT_ps[:, n % 2, :],
                                 ACT.Copy).then_inc(s_hhi, 1)

                def gelu_bank(n):
                    hb = hid[:, n * BANK:(n + 1) * BANK]
                    act.wait_ge(s_z, s * NB + n + 1)
                    a.activation(hb, hb, ACT.Gelu).then_inc(s_gelu, 1)
                    act.wait_ge(s_gelu, s * NB + n + 1)
                    a.activation(hb, hb, ACT.Copy, scale=SH).then_inc(s_hs, 1)

                if there(s, -1, inner):
                    hi_group(0)
                    hi_group(1)
                if there(s, 1, inner):
                    act.wait_ge(s_xT, s + 2)
                    a.activation(xT16[:, 0].rearrange("p k t -> p (k t)"), xT_ps[:],
                                 ACT.Copy).then_inc(s_xhi, 1)
                if there(s, -2, inner):
                    b = slot_value(act, BATCH, s - 2, S - 1)
                    act.wait_ge(s_done, s)
                    act.dma_start(out[bass.ds(b, 1), :, :].rearrange("a t n -> t (a n)"),
                                  y[:]).then_inc(s_y, 16)
                if there(s, 0, inner):
                    gelu_bank(0)
                if there(s, -1, inner):
                    hi_group(2)
                if there(s, 0, inner):
                    gelu_bank(1)
                if there(s, -1, inner):
                    hi_group(3)
                if there(s, 0, inner):
                    gelu_bank(2)
                    gelu_bank(3)

            load_x(0, slot_value(act, BATCH, 0, S - 1))
            raws = [w[:, 1].rearrange("p a k n -> p (a k n)").bitcast(F32) for w in (wi16, wo16)]
            his = [w[:, 0, 0].rearrange("p k n -> p (k n)") for w in (wi16, wo16)]
            drop = z_ps[:].rearrange("p b n -> p (b n)")

            def squares(src, n):
                chain.step(a.activation(drop, src, ACT.Square, accum_out=boot_ss[:, n:n + 1]))
                a.nop().then_inc(s_bsq, 1)

            def hi_parts(m):
                act.wait_ge(s_bscale, (1, 3)[m])
                for q in range(Q):
                    c = slice(q * QN, (q + 1) * QN)
                    a.activation(his[m][:, c], raws[m][:, c], ACT.Copy,
                                 scale=wscale[:, m:m + 1]).then_inc(s_bhi, 1)

            for q in range(Q):
                act.wait_ge(s_braw[q], 16)
                squares(raws[0][:, q * QN:(q + 1) * QN], q)
            act.wait_ge(s_bias[0], 64)
            squares(bi_all[:, 0, :], 2 * Q + 1)
            hi_parts(0)
            for q in range(Q):
                act.wait_ge(s_braw[Q + q], 16)
                squares(raws[1][:, q * QN:(q + 1) * QN], Q + q)
            hi_parts(1)

            pipeline(act, iteration)
            act.wait_ge(s_y, 16 * S)

        @block.vector
        def _(dve):
            v = nc.vector
            chain = Steps(dve, s_dve)
            step = chain.step
            v.memset(ones, 1.0).then_inc(s_done, 1)
            dve.wait_ge(s_idx, 64)
            dve.wait_ge(s_iota, 1)

            turns, r = angle[:, 4:6], angle[:, 8:10]
            step(v.tensor_scalar(turns, angle[:, 0:2], 1.0 / 6.283185307179586, TO_INTEGER, ALU.mult, ALU.add))
            step(v.tensor_scalar(turns, turns, -TO_INTEGER, None, ALU.add))
            step(v.tensor_copy(r, angle[:, 0:2]))
            for part in TWO_PI_PARTS:
                step(v.scalar_tensor_tensor(out=r, in0=turns, scalar=-part, in1=r, op0=ALU.mult, op1=ALU.add))
            step(v.tensor_scalar(angle[:, 18:20], r, BELOW_PI, -BELOW_PI, ALU.min, ALU.max))
            step(v.scalar_tensor_tensor(out=r, in0=angle[:, 18:20], scalar=-1.0, in1=angle[:, 18:20],
                                        op0=ALU.mult, op1=ALU.max))
            v.tensor_scalar(angle[:, 16:18], r, -1.0, 1.5707963267948966, ALU.mult, ALU.add).then_inc(s_ang, 1)

            step(v.tensor_copy(keys_e, keys_i))
            step(v.tensor_copy(iota_f, iota_i))
            step(v.tensor_scalar(keys_k, keys_e, 0.0, float(E), ALU.is_lt, ALU.mult))
            step(v.tensor_tensor(keys_e, keys_e, keys_k, ALU.add))
            step(v.tensor_scalar(keys_e, keys_e, 0.0, E - 1.0, ALU.max, ALU.min))
            step(v.scalar_tensor_tensor(out=keys_k, in0=keys_e, scalar=float(S), in1=iota_f, op0=ALU.mult, op1=ALU.add))
            pos, start, first, rank, fe = (cols[:, j:j + 1] for j in range(5))
            e_col, k_col, i_col = keys_e[:, S:S + 1], keys_k[:, S:S + 1], iota_f[:, S:S + 1]
            step(v.tensor_scalar(less, keys_k[:, 0:S], k_col, None, ALU.is_lt))
            step(v.reduce_sum(pos, less, AX.X))
            step(v.tensor_scalar(less, keys_e[:, 0:S], e_col, None, ALU.is_lt))
            step(v.reduce_sum(start, less, AX.X))
            step(v.tensor_tensor(first, pos, start, ALU.is_equal))
            step(v.tensor_tensor(fe, first, e_col, ALU.mult))
            step(v.tensor_scalar(onehot, iota_f[:, 0:S], pos, None, ALU.is_equal))
            v.tensor_scalar(less, keys_e[:, 0:S], e_col, None, ALU.is_gt).then_inc(s_less, 1)
            dve.wait_ge(s_rankp, 1)
            step(v.tensor_copy(rank, xT_ps[:, 0:1]))
            step(v.tensor_scalar(onehot_r, iota_f[:, 0:E], rank, None, ALU.is_equal))
            step(v.tensor_scalar(after_r, iota_f[:, 0:E + 1], rank, None, ALU.is_gt))
            v.engine_nop().then_inc(s_onehot, 1)
            dve.wait_ge(s_tabp, 1)
            v.tensor_copy(tab[0:1, BATCH:BATCH + S], xT_ps[0:1, 0:S])
            v.tensor_copy(tab[0:1, RANK:RANK + S], xT_ps[0:1, S:2 * S])
            v.tensor_copy(tab[0:1, EXPERT:EXPERT + E], xT_ps[0:1, 2 * S:2 * S + E])
            step(v.tensor_scalar(tab[0:1, BEFORE:BEFORE + E + 1], xT_ps[0:1, 3 * S:3 * S + E + 1], 1.0, None, ALU.add))
            step(v.tensor_scalar(tab[0:1, BUF:BUF + S], tab[0:1, RANK:RANK + S], 1, None, ALU.bitwise_and))
            v.engine_nop().then_inc(s_tables, 1)

            dve.wait_ge(s_sin, 1)
            for j in range(4):
                step(v.tensor_copy(spread[:, j * P:(j + 1) * P], angle[:, 20 + j:21 + j].to_broadcast([P, P])))
            v.engine_nop().then_inc(s_onehot, 1)
            dve.wait_ge(s_tabp, 2)
            for col, src, sign in ((0, 0, 1), (1, 0, 1), (2, 1, 1), (3, 1, 1), (4, 2, -1), (5, 2, 1), (6, 3, -1), (7, 3, 1)):
                step(v.tensor_scalar(rot[:, :, col], o_ps[:, src * S:(src + 1) * S], float(sign), None, ALU.mult))

            def row(tile, b, cols=slice(None)):
                return tile[:, bass.ds(b, 1), cols].rearrange("p a n -> p (a n)")

            def as_int(ap):
                return ap.bitcast(I32)

            def scale_x(s, inner):
                dve.wait_ge(s_sq, s + 1)
                if inner or s >= 1:
                    dve.wait_ge(s_xs, s)
                step(v.tensor_scalar(as_int(TM), as_int(SS), 24, None, ALU.logical_shift_right))
                step(v.tensor_scalar(as_int(row(inv, s % XB, slice(ISX, ISX + 1))), as_int(TM),
                                     float(EXP1), float(INVERSE * EXP1), ALU.mult, ALU.add))
                v.tensor_scalar(as_int(SX), as_int(TM), float(-EXP1), float(SCALE * EXP1),
                                ALU.mult, ALU.add).then_inc(s_sx, 1)

            def scale_h(s, b, inner):
                if inner or s >= 1:
                    dve.wait_ge(s_hs, s * NB)
                isx = row(inv, s % XB, slice(ISX, ISX + 1))
                ish = row(inv, s % XB, slice(ISH, ISH + 1))
                of = lambda k: row(ex, b, slice(k, k + 1))
                step(v.tensor_scalar(TB, isx, of(AWI), of(NBI), ALU.mult, ALU.add))
                step(v.tensor_scalar(as_int(TM), as_int(TB), 23, None, ALU.logical_shift_right))
                step(v.tensor_scalar(as_int(SH), as_int(TM), float(-EXP1), float(SCALE_F * EXP1), ALU.mult, ALU.add))
                step(v.tensor_scalar(as_int(ish), as_int(TM), float(EXP1), float(INVERSE_F * EXP1), ALU.mult, ALU.add))
                step(v.tensor_tensor(ZS, isx, of(IWI), ALU.mult))

            def z_bank(s, n, b, inner):
                dve.wait_ge(s_g1, s * NB + n + 1)
                if inner or s >= 1:
                    dve.wait_ge(s_hT, (s - 1) * NB + n + 1)
                hb = slice(n * BANK, (n + 1) * BANK)
                v.scalar_tensor_tensor(out=hid[:, hb], in0=z_ps[:, n, :], scalar=ZS,
                                       in1=row(bi_all, b, hb), op0=ALU.mult, op1=ALU.add).then_inc(s_z, 1)

            def lo_group(s, n):
                dve.wait_ge(s_hhi, (s) * NB + n + 1)
                v.tensor_tensor(hT16[:, n % 2, 1].rearrange("p c t -> p (c t)"), hT_ps[:, n % 2, :],
                                hT16[:, n % 2, 0].rearrange("p c t -> p (c t)"), ALU.subtract).then_inc(s_hlo, 1)

            os, mean, var, t, rstd = ln[:, 0:1], ln[:, 1:2], ln[:, 2:3], ln[:, 3:4], ln[:, 4:5]

            def residual(s, b, inner):
                dve.wait_ge(s_g2, (s + 1) * NB)
                if inner or s >= 1:
                    dve.wait_ge(s_y, s * 16)
                step(v.tensor_tensor(os, row(inv, s % XB, slice(ISH, ISH + 1)), row(ex, b, slice(IWO, IWO + 1)), ALU.mult))
                v.scalar_tensor_tensor(out=y[:], in0=o_ps[:], scalar=os, in1=row(xbuf, s % XB), op0=ALU.mult, op1=ALU.add).then_inc(s_res, 1)

            def finish(s, b):
                bgb = lambda j: bgb_all[:, bass.ds(b, 1), j, :].rearrange("p a n -> p (a n)")
                dve.wait_ge(s_res, s + 1)
                step(v.tensor_tensor(y[:], y[:], bgb(0), ALU.add))
                step(v.bn_stats(ln[:, 8:14], y[:]))
                step(v.bn_aggr(ln[:, 1:3], ln[:, 8:14]))
                step(v.tensor_scalar(var, var, LN_EPS, None, ALU.add))
                step(v.tensor_scalar(as_int(t), as_int(var), 1, None, ALU.logical_shift_right))
                step(v.tensor_scalar(as_int(rstd), as_int(t), -1.0, float(0x5F3759DF), ALU.mult, ALU.add))
                for _ in range(3):
                    step(v.scalar_tensor_tensor(out=t, in0=rstd, scalar=var, in1=rstd, op0=ALU.mult, op1=ALU.mult))
                    step(v.tensor_scalar(t, t, -0.5, 1.5, ALU.mult, ALU.add))
                    step(v.tensor_tensor(rstd, rstd, t, ALU.mult))
                step(v.tensor_scalar(y[:], y[:], mean, rstd, ALU.subtract, ALU.mult))
                step(v.tensor_tensor(y[:], y[:], bgb(1), ALU.mult))
                step(v.tensor_tensor(y[:], y[:], bgb(2), ALU.add))
                quads = lambda ap: ap.rearrange("p (d f) -> p d f", f=4)
                table = lambda k: rot[:, bass.ds(s, 1), k:k + 4].to_broadcast([P, H // 4, 4])
                step(v.tensor_tensor(quads(turned[:]), quads(y[:]), table(4), ALU.mult))
                step(v.tensor_tensor(quads(y[:]), quads(y[:]), table(0), ALU.mult))
                pairs = lambda ap: ap.rearrange("p (d f) -> p d f", f=2)
                step(v.tensor_tensor(pairs(y[:])[:, :, 0], pairs(y[:])[:, :, 0], pairs(turned[:])[:, :, 1], ALU.add))
                v.tensor_tensor(pairs(y[:])[:, :, 1], pairs(y[:])[:, :, 1], pairs(turned[:])[:, :, 0], ALU.add).then_inc(s_done, 1)

            def iteration(s, inner=False):
                chain.clear()
                if there(s, -2, inner):
                    b2 = slot_value(dve, BUF, s - 2, 1)
                    residual(s - 2, b2, inner)
                if there(s, 1, inner):
                    scale_x(s + 1, inner)
                if there(s, -2, inner):
                    finish(s - 2, b2)
                if there(s, 0, inner):
                    b = slot_value(dve, BUF, s, 1)
                    dve.wait_ge(s_wi, slot_value(dve, RANK, s, E - 1) + 1)
                    scale_h(s, b, inner)
                if there(s, -1, inner):
                    lo_group(s - 1, 0)
                    lo_group(s - 1, 1)
                if there(s, 1, inner):
                    dve.wait_ge(s_xhi, s + 2)
                    v.tensor_tensor(xT16[:, 1].rearrange("p k t -> p (k t)"), xT_ps[:],
                                    xT16[:, 0].rearrange("p k t -> p (k t)"), ALU.subtract).then_inc(s_xlo, 1)
                if there(s, 0, inner):
                    z_bank(s, 0, b, inner)
                if there(s, -1, inner):
                    lo_group(s - 1, 2)
                if there(s, 0, inner):
                    z_bank(s, 1, b, inner)
                if there(s, -1, inner):
                    lo_group(s - 1, 3)
                if there(s, 0, inner):
                    z_bank(s, 2, b, inner)
                    z_bank(s, 3, b, inner)

            raws = [w[:, 1].rearrange("p a k n -> p (a k n)").bitcast(F32) for w in (wi16, wo16)]
            his = [w[:, 0, 0].rearrange("p k n -> p (k n)") for w in (wi16, wo16)]
            los = [w[:, 0, 1].rearrange("p k n -> p (k n)") for w in (wi16, wo16)]

            def total(m):
                step(v.reduce_sum(boot_ss[:, 2 * Q + 2 * m:2 * Q + 2 * m + 1], boot_ss[:, m * Q:(m + 1) * Q], AX.X))
                v.engine_nop().then_inc(s_bsum, 1)

            def lo_parts(m):
                for q in range(Q):
                    c = slice(q * QN, (q + 1) * QN)
                    dve.wait_ge(s_bhi, m * Q + q + 1)
                    step(v.scalar_tensor_tensor(out=los[m][:, c], in0=raws[m][:, c], scalar=wscale[:, m:m + 1],
                                                in1=his[m][:, c], op0=ALU.mult, op1=ALU.subtract))
                v.engine_nop().then_inc((s_wi, s_wo)[m], 1)

            dve.wait_ge(s_bsq, Q)
            total(0)
            dve.wait_ge(s_bsq, Q + 1)
            v.engine_nop().then_inc(s_bsum, 1)
            dve.wait_ge(s_bscale, 2)
            lo_parts(0)
            dve.wait_ge(s_bsq, 2 * Q + 1)
            total(1)
            dve.wait_ge(s_bscale, 3)
            lo_parts(1)

            pipeline(dve, iteration)

        @block.tensor
        def _(pe):
            t = nc.tensor
            fe, first, rank = cols[:, 4:5], cols[:, 2:3], cols[:, 3:4]
            pe.wait_ge(s_less, 1)
            t.matmul(xT_ps[:, 0:1], less, first, start=True, stop=True).then_inc(s_rankp, 1)
            pe.wait_ge(s_onehot, 1)
            t.matmul(xT_ps[0:1, 0:S], iota_f[:, S:S + 1], onehot, start=True, stop=True)
            t.matmul(xT_ps[0:1, S:2 * S], rank, onehot, start=True, stop=True)
            t.matmul(xT_ps[0:1, 2 * S:2 * S + E], fe, onehot_r, start=True, stop=True)
            t.matmul(xT_ps[0:1, 3 * S:3 * S + E + 1], ones, after_r, start=True, stop=True).then_inc(s_tabp, 1)
            pe.wait_ge(s_onehot, 2)
            for j in range(4):
                last = t.matmul(o_ps[:, j * S:(j + 1) * S], spread[:, j * P:(j + 1) * P], onehot, start=True, stop=True)
            last.then_inc(s_tabp, 1)
            pe.wait_ge(s_tables, 1)
            pe.wait_ge(s_ident, 1)

            PASSES = ((1, 0), (0, 1), (0, 0))

            def transpose_h(s, n, inner):
                G = s * NB + n
                pe.wait_ge(s_hs, G + 1)
                if inner or G >= 2:
                    pe.wait_ge(s_hlo, G - 1)
                for c in range(GC):
                    last = t.transpose(hT_ps[:, n % 2, c * P:(c + 1) * P],
                                       hid[:, (n * GC + c) * P:(n * GC + c + 1) * P], ident[:])
                last.then_inc(s_hT, 1)

            def first_product(s, n, b, inner):
                if inner or s >= 1:
                    pe.wait_ge(s_z, (s - 1) * NB + n + 1)
                cs = slice(n * BANK, (n + 1) * BANK)
                for k in range(KH):
                    for a, w in PASSES:
                        last = t.matmul(z_ps[:, n, :], xT16[:, a, k, :], wi16[:, bass.ds(b, 1), w, k, cs],
                                        start=(k == 0 and (a, w) == PASSES[0]),
                                        stop=(k == KH - 1 and (a, w) == PASSES[-1]))
                last.then_inc(s_g1, 1)

            def second_product(s, n, b):
                pe.wait_ge(s_hlo, s * NB + n + 1)
                for c in range(GC):
                    for a, w in PASSES:
                        last = t.matmul(o_ps[:], hT16[:, n % 2, a, c, :], wo16[:, bass.ds(b, 1), w, n * GC + c, :],
                                        start=(n == 0 and c == 0 and (a, w) == PASSES[0]),
                                        stop=(n == NB - 1 and c == GC - 1 and (a, w) == PASSES[-1]))
                last.then_inc(s_g2, 1)

            def iteration(s, inner=False):
                if there(s, 0, inner):
                    b = slot_value(pe, BUF, s, 1)
                    pe.wait_ge(s_wi, slot_value(pe, RANK, s, E - 1) + 1)
                    pe.wait_ge(s_xlo, s + 1)
                    for n in range(NB - 1):
                        first_product(s, n, b, inner)
                if there(s, -1, inner):
                    transpose_h(s - 1, 0, inner)
                if there(s, 0, inner):
                    first_product(s, NB - 1, b, inner)
                if there(s, -1, inner):
                    transpose_h(s - 1, 1, inner)
                if there(s, 1, inner):
                    pe.wait_ge(s_xs, s + 2)
                    for k in range(KH):
                        last = t.transpose(xT_ps[:, k * P:(k + 1) * P], xs[:, k * P:(k + 1) * P], ident[:])
                    last.then_inc(s_xT, 1)
                if there(s, -1, inner):
                    b1 = slot_value(pe, BUF, s - 1, 1)
                    pe.wait_ge(s_wo, slot_value(pe, RANK, s - 1, E - 1) + 1)
                    if inner or s >= 2:
                        pe.wait_ge(s_res, s - 1)
                    second_product(s - 1, 0, b1)
                    transpose_h(s - 1, 2, inner)
                    second_product(s - 1, 1, b1)
                    transpose_h(s - 1, 3, inner)
                    second_product(s - 1, 2, b1)
                    second_product(s - 1, 3, b1)

            pipeline(pe, iteration)


_INS = ["x", "itok_B_0_7", "condB_theta", "condB_phi", "L0_cond_Wi", "L0_cond_bi", "L0_cond_Wo",
        "L0_cond_bo", "L0_cond_gamma", "L0_cond_beta"]


def kernel(**inputs):
    import numpy as np
    import concourse.bacc as bacc
    from concourse import mybir as mb
    from concourse.bass_utils import run_bass_kernel_spmd

    nc = bacc.Bacc("TRN2", target_bir_lowering=False, num_devices=1)
    arrays, args = {}, []
    for name in _INS:
        a = np.ascontiguousarray(inputs[name])
        arrays[f"in_{name}"] = a
        args.append(nc.dram_tensor(f"in_{name}", a.shape, mb.dt.from_np(a.dtype), kind="ExternalInput").ap())
    shape = arrays["in_x"].shape
    args.append(nc.dram_tensor("out", shape, mb.dt.float32, kind="ExternalOutput").ap())
    expert_mlp_rotate_kernel(nc, *args)
    result = run_bass_kernel_spmd(nc, [arrays], core_ids=[0])
    return result.results[0]["out"]
```

```python
import concourse.bass as bass
from concourse import mybir
from contextlib import ExitStack

F32 = mybir.dt.float32
F16 = mybir.dt.float16
I32 = mybir.dt.int32
ALU = mybir.AluOpType
ACT = mybir.ActivationFunctionType
AX = mybir.AxisListType
ADD_LANES = bass.bass_isa.ReduceOp.add

P = 128
BANK = 512
LN_EPS = 1e-12
EXP1 = 1 << 23
EXP2 = 1 << 24
SCALE, INVERSE, BOUND = 204, 50, 65
SCALE_F, INVERSE_F = 268, -14
TWO_PI_PARTS = (6.28125, 0.0019350051879882812, 3.0199159819567e-07)
TO_INTEGER = 1.5 * 2.0 ** 23
BELOW_PI = 3.1415925


class Steps:

    def __init__(self, engine, sem):
        self.engine, self.sem, self.n = engine, sem, 0

    def step(self, ins):
        ins.then_inc(self.sem, 1)
        self.n += 1
        self.engine.wait_ge(self.sem, self.n)

    def clear(self):
        self.engine.sem_clear(self.sem)
        self.n = 0


def expert_mlp_rotate_kernel(nc, x, itok, theta, phi, Wi, bi, Wo, bo, gamma, beta, out):
    S, T, H = x.shape
    E, _, I = Wi.shape
    KH, KI = H // P, I // P
    NB = I // BANK
    GC = KI // NB
    Q = 4
    QN = H * I // P // Q
    XB = 8
    RB = 3
    assert T == P and S == P and H == BANK and E % 2 == 0 and NB == Q == KH

    ctx = ExitStack()
    with ctx:
        def sb(name, shape, dt=F32):
            return ctx.enter_context(nc.sbuf_tensor(name, shape, dt))

        def pb(name, shape, dt=F32):
            return ctx.enter_context(nc.psum_tensor(name, shape, dt))

        def sem(name):
            return ctx.enter_context(nc.semaphore(name))

        wi16 = sb("wi16", [P, 2, 2, KH, I], F16)
        wo16 = sb("wo16", [P, 2, 2, KI, H], F16)
        staged = sb("staged", [P, 2, QN])
        bi_all = sb("bi_all", [P, 2, I])
        bgb_all = sb("bgb_all", [P, RB, 3, H])
        hid = sb("hid", [P, I])
        hT16 = sb("hT16", [P, 2, 2, GC, P], F16)
        xbuf = sb("xbuf", [P, XB, H])
        xs = sb("xs", [P, H])
        xT16 = sb("xT16", [P, 2, KH, P], F16)
        y = sb("y", [P, H])
        turned = sb("turned", [P, H])
        rot = sb("rot", [P, S, 8])
        ident = sb("ident", [P, P])
        tab = sb("tab", [1, 4 * S + 2 * E + 1], I32)
        BATCH, RANK, BUF, BUF3, EXPERT, BEFORE = 0, S, 2 * S, 3 * S, 4 * S, 4 * S + E
        tok = sb("tok", [P, 6])
        SS, SX, SH, ZS, TM, TB = (tok[:, j:j + 1] for j in range(6))
        inv = sb("inv", [P, XB, 2])
        ISX, ISH = range(2)
        ex = sb("ex", [P, 2, 4])
        IWI, AWI, NBI, IWO = range(4)
        wscale = sb("wscale", [P, 2])
        ln = sb("ln", [P, 16])
        consts = sb("consts", [P, 6], I32)
        pool_s = sb("pool_s", [P, 4])
        boot_ss = sb("boot_ss", [P, 2 * Q + 3])

        z_ps = pb("z_ps", [P, NB, BANK])
        hT_ps = pb("hT_ps", [P, 2, BANK])
        xT_ps = pb("xT_ps", [P, BANK])
        o_ps = pb("o_ps", [P, BANK])

        keys_i = hid[:, 0:129].bitcast(I32)
        iota_i = hid[:, 132:261].bitcast(I32)
        keys_e = hid[:, 264:393]
        keys_k = hid[:, 396:525]
        iota_f = hid[:, 528:657]
        less = hid[:, 660:788]
        onehot = hid[:, 792:920]
        onehot_r = hid[:, 924:924 + E]
        after_r = hid[:, 940:940 + E + 1]
        ones = hid[:, 960:961]
        cols = hid[:, 964:980]
        angle = hid[:, 980:1010]
        spread = hid[:, 1024:1024 + 4 * P]

        s_idx = sem("s_idx")
        s_iota = sem("s_iota")
        s_ident = sem("s_ident")
        s_pool = sem("s_pool")
        s_dve = sem("s_dve")
        s_act = sem("s_act")
        s_ang = sem("s_ang")
        s_sin = sem("s_sin")
        s_less = sem("s_less")
        s_rankp = sem("s_rankp")
        s_onehot = sem("s_onehot")
        s_tabp = sem("s_tabp")
        s_tables = sem("s_tables")
        s_braw = [sem(f"s_braw{i}") for i in range(2 * Q)]
        s_bsq = sem("s_bsq")
        s_bsum = sem("s_bsum")
        s_bscale = sem("s_bscale")
        s_bhi = sem("s_bhi")
        s_bias = [sem(f"s_bias{i}") for i in range(2)]
        s_stage = [sem(f"s_stage{i}") for i in range(2)]
        s_unstage = [sem(f"s_unstage{i}") for i in range(2)]
        s_wi = sem("s_wi")
        s_wo = sem("s_wo")
        s_x = sem("s_x")
        s_y = sem("s_y")
        s_sq = sem("s_sq")
        s_sx = sem("s_sx")
        s_xs = sem("s_xs")
        s_xT = sem("s_xT")
        s_xhi = sem("s_xhi")
        s_xlo = sem("s_xlo")
        s_g1 = sem("s_g1")
        s_z = sem("s_z")
        s_gelu = sem("s_gelu")
        s_hs = sem("s_hs")
        s_hT = sem("s_hT")
        s_hhi = sem("s_hhi")
        s_hlo = sem("s_hlo")
        s_g2 = sem("s_g2")
        s_res = sem("s_res")
        s_ln = sem("s_ln")
        s_done = sem("s_done")

        block = ctx.enter_context(nc.Block())

        def slot_value(engine, table, s, top, least=0):
            return engine.value_load(tab[0:1, bass.ds(s + table, 1)], min_val=least, max_val=top)

        def pipeline(engine, iteration):
            iteration(-1)
            iteration(0)
            iteration(1)
            iteration(2)
            with engine.Fori(3, S - 2) as s:
                iteration(s, True)
            for s in range(S - 2, S + 2):
                iteration(s)

        def there(s, d, inner):
            return inner or 0 <= s + d < S

        @block.sync
        def _(sp):
            sp.dma_start(keys_i[:, 0:S], itok.partition_broadcast(P)).then_inc(s_idx, 16)
            sp.dma_start(keys_i[:, S:S + 1], itok.rearrange("(p o) -> p o", o=1)).then_inc(s_idx, 16)
            sp.dma_start(angle[:, 0:1], theta.rearrange("(p o) -> p o", o=1)).then_inc(s_idx, 16)
            sp.dma_start(angle[:, 1:2], phi.rearrange("(p o) -> p o", o=1)).then_inc(s_idx, 16)

            def weight_quarter(m, e, q):
                if m == 0:
                    return Wi[bass.ds(e, 1), q * P:(q + 1) * P, :].rearrange("e p n -> p (e n)")
                rows = slice(q * GC * P, (q + 1) * GC * P)
                return Wo[bass.ds(e, 1), rows, :].rearrange("e (c p) n -> p (e c) n", p=P)

            def quarter_view(region, m):
                return region if m == 0 else region.rearrange("p (c n) -> p c n", n=H)

            def load_biases(e, b, b3):
                sp.dma_start(bi_all[:, b, :], bi[bass.ds(e, 1), :].broadcast_to([P, I])).then_inc(s_bias[b], 16)
                for j, v in enumerate((bo, gamma, beta)):
                    sp.dma_start(bgb_all[:, b3, j, :], v[bass.ds(e, 1), :].broadcast_to([P, H])).then_inc(s_bias[b], 16)

            sp.wait_ge(s_tables, 1)
            e0 = slot_value(sp, EXPERT, 0, E - 1)
            for m, w in enumerate((wi16, wo16)):
                raw = w[:, 1].rearrange("p a k n -> p (a k n)").bitcast(F32)
                for q in range(Q):
                    sp.dma_start(quarter_view(raw[:, q * QN:(q + 1) * QN], m),
                                 weight_quarter(m, e0, q)).then_inc(s_braw[m * Q + q], 16)
                if m == 0:
                    load_biases(e0, 0, 0)

            def rank(r, b, nth):
                e = slot_value(sp, EXPERT, r, E - 1)
                if isinstance(r, int) and r == 1:
                    load_biases(e, b, r)
                else:
                    sp.wait_ge(s_res, slot_value(sp, BEFORE, r - 1, S, 1))
                    load_biases(e, b, bass.ds(r % RB, 1))
                j = 0
                for m in range(2):
                    for again in range(2):
                        for q in range(Q):
                            used = (r - 1) * (2 * Q) + j // 2
                            if not isinstance(used, int) or used > 0:
                                sp.wait_ge(s_unstage[j % 2], used)
                            sp.dma_start(quarter_view(staged[:, j % 2, :], m),
                                         weight_quarter(m, e, q)).then_inc(s_stage[j % 2], 16)
                            j += 1

            rank(1, 1, 0)
            with sp.Fori(1, E // 2) as i:
                rank(i * 2, 0, i)
                rank(i * 2 + 1, 1, i)

        @block.gpsimd
        def _(pool):
            g = nc.gpsimd
            chain = Steps(pool, s_pool)
            g.iota(iota_i[:, 0:S], [[1, S]], base=0, channel_multiplier=0)
            g.iota(iota_i[:, S:S + 1], [[1, 1]], base=0, channel_multiplier=1)
            for j, c in enumerate((EXP2, EXP1, SCALE * EXP1, INVERSE * EXP1, (INVERSE + 30) * EXP1,
                                   BOUND * EXP1)):
                last = g.memset(consts[:, j:j + 1], c)
            last.then_inc(s_iota, 1)
            chain.step(g.memset(ident[:], 0.0))
            g.affine_select(out=ident[:], in_=ident[:], compare_op=ALU.not_equal, fill=1.0, base=0,
                            pattern=[[-1, P]], channel_multiplier=1).then_inc(s_ident, 1)

            def scale_of(ss, scale_out, outs, chain):
                c = consts
                chain.step(g.tensor_tensor(pool_s[:, 1:2].bitcast(I32), ss.bitcast(I32), c[:, 0:1], ALU.divide))
                chain.step(g.tensor_tensor(pool_s[:, 2:3].bitcast(I32), pool_s[:, 1:2].bitcast(I32), c[:, 1:2], ALU.mult))
                t = pool_s[:, 2:3].bitcast(I32)
                if scale_out is not None:
                    chain.step(g.tensor_tensor(scale_out.bitcast(I32), c[:, 2:3], t, ALU.subtract))
                for o, j in outs:
                    chain.step(g.tensor_tensor(o.bitcast(I32), t, c[:, j:j + 1], ALU.add))

            def scales(what, ss, b, chain):
                col = lambda k: ex[:, b, k:k + 1]
                if what == "wi":
                    scale_of(ss, wscale[:, 0:1], [(col(IWI), 3), (col(AWI), 4)], chain)
                elif what == "wo":
                    scale_of(ss, wscale[:, 1:2], [(col(IWO), 3)], chain)
                else:
                    scale_of(ss, None, [(col(NBI), 5)], chain)

            for n, what in enumerate(("wi", "bi", "wo")):
                pool.wait_ge(s_bsum, n + 1)
                ss = boot_ss[:, 2 * Q + n:2 * Q + n + 1]
                if what != "bi":
                    chain.step(g.partition_all_reduce(pool_s[:, 0:1], ss, P, ADD_LANES))
                    ss = pool_s[:, 0:1]
                scales(what, ss, 0, chain)
                g.engine_nop().then_inc(s_bscale, 1)

            PIECE = 1024
            def rank(r, b, nth):
                chain.clear()
                boot = isinstance(r, int) and r == 1
                before = None if boot else slot_value(pool, BEFORE, r - 1, S, 1)

                def quarter(j):
                    pool.wait_ge(s_stage[j % 2], 16)
                    pool.sem_clear(s_stage[j % 2])
                    return staged[:, j % 2, :]

                def fold(acc):
                    w = QN // 2
                    while w:
                        chain.step(g.tensor_tensor(acc[:, 0:w], acc[:, 0:w], acc[:, w:2 * w], ALU.add))
                        w //= 2
                    return acc[:, 0:1]

                j = 0
                for m, w in enumerate((wi16, wo16)):
                    hi = w[:, b, 0].rearrange("p k n -> p (k n)")
                    lo = w[:, b, 1].rearrange("p k n -> p (k n)")
                    room = lo.bitcast(F32)
                    acc, sq = room[:, 0:QN], room[:, QN:2 * QN]
                    for q in range(Q):
                        raw = quarter(j)
                        if j == 0 and boot:
                            pool.wait_ge(s_wo, 1)
                        elif j == 0:
                            pool.wait_ge(s_res, before)
                        for at in range(0, QN, PIECE):
                            p = slice(at, at + PIECE)
                            to = (acc if q == 0 else sq)[:, p]
                            ins = g.tensor_tensor(to, raw[:, p], raw[:, p], ALU.mult)
                            chain.step(ins)
                            if q:
                                chain.step(g.tensor_tensor(acc[:, p], acc[:, p], sq[:, p], ALU.add))
                        g.engine_nop().then_inc(s_unstage[j % 2], 1)
                        j += 1
                    fold(acc)
                    chain.step(g.partition_all_reduce(pool_s[:, 0:1], acc[:, 0:1], P, ADD_LANES))
                    scales(("wi", "wo")[m], pool_s[:, 0:1], b, chain)
                    if m == 0:
                        pool.wait_ge(s_bias[b], nth * 64 + 64)
                        chain.step(g.tensor_tensor(acc, bi_all[:, b, :], bi_all[:, b, :], ALU.mult))
                        fold(acc)
                        scales("bi", acc[:, 0:1], b, chain)
                    for q in range(Q):
                        raw = quarter(j)
                        for at in range(0, QN, PIECE):
                            p, o = slice(at, at + PIECE), slice(q * QN + at, q * QN + at + PIECE)
                            s = wscale[:, m:m + 1]
                            chain.step(g.tensor_scalar(hi[:, o], raw[:, p], s, 1.0, ALU.mult, ALU.mult))
                            chain.step(g.tensor_scalar(raw[:, p], raw[:, p], s, 1.0, ALU.mult, ALU.mult))
                            chain.step(g.tensor_tensor(lo[:, o], raw[:, p], hi[:, o], ALU.subtract))
                        g.engine_nop().then_inc(s_unstage[j % 2], 1)
                        j += 1
                    g.engine_nop().then_inc((s_wi, s_wo)[m], 1)

            rank(1, 1, 0)
            with pool.Fori(1, E // 2) as i:
                rank(i * 2, 0, i)
                rank(i * 2 + 1, 1, i)

        @block.scalar
        def _(act):
            a = nc.scalar
            chain = Steps(act, s_act)
            act.wait_ge(s_ang, 1)
            a.activation(angle[:, 20:24], angle[:, 16:20], ACT.Sin).then_inc(s_sin, 1)
            act.wait_ge(s_tables, 1)

            def load_x(s, b):
                act.dma_start(xbuf[:, bass.ds(s % XB, 1), :].rearrange("p a n -> p (a n)"),
                              x[bass.ds(b, 1), :, :].rearrange("a t n -> t (a n)")).then_inc(s_x, 16)

            def iteration(s, inner=False):
                if there(s, 2, inner):
                    b = slot_value(act, BATCH, s + 2, S - 1)
                if there(s, 1, inner):
                    act.wait_ge(s_x, (s + 2) * 16)
                    if inner or s >= 0:
                        act.wait_ge(s_xT, s + 1)
                if there(s, 2, inner):
                    if inner or s >= 3:
                        act.wait_ge(s_done, s - 2)
                    load_x(s + 2, b)
                if there(s, 1, inner):
                    xv = xbuf[:, bass.ds((s + 1) % XB, 1), :].rearrange("p a n -> p (a n)")
                    a.activation(xs[:], xv, ACT.Square, accum_out=SS).then_inc(s_sq, 1)
                    act.wait_ge(s_sx, 1)
                    act.sem_clear(s_sx)
                    a.activation(xs[:], xv, ACT.Copy, scale=SX).then_inc(s_xs, 1)

                def hi_group(n):
                    G = (s - 1) * NB + n
                    act.wait_ge(s_hT, G + 1)
                    if inner or G >= 2:
                        act.wait_ge(s_g2, G - 1)
                    a.activation(hT16[:, n % 2, 0].rearrange("p c t -> p (c t)"), hT_ps[:, n % 2, :],
                                 ACT.Copy).then_inc(s_hhi, 1)

                def gelu_bank(n):
                    hb = hid[:, n * BANK:(n + 1) * BANK]
                    act.wait_ge(s_z, s * NB + n + 1)
                    a.activation(hb, hb, ACT.Gelu).then_inc(s_gelu, 1)
                    act.wait_ge(s_gelu, s * NB + n + 1)
                    a.activation(hb, hb, ACT.Copy, scale=SH).then_inc(s_hs, 1)

                back, here = there(s, -1, inner), there(s, 0, inner)
                if back:
                    hi_group(0)
                if here:
                    gelu_bank(0)
                if back:
                    hi_group(1)
                if there(s, 1, inner):
                    act.wait_ge(s_xT, s + 2)
                    a.activation(xT16[:, 0].rearrange("p k t -> p (k t)"), xT_ps[:],
                                 ACT.Copy).then_inc(s_xhi, 1)
                if back:
                    hi_group(2)
                if here:
                    gelu_bank(1)
                if back:
                    hi_group(3)
                if here:
                    gelu_bank(2)
                    gelu_bank(3)
                if there(s, -2, inner):
                    b = slot_value(act, BATCH, s - 2, S - 1)
                    act.wait_ge(s_done, s - 1)
                    act.dma_start(out[bass.ds(b, 1), :, :].rearrange("a t n -> t (a n)"),
                                  y[:]).then_inc(s_y, 16)

            load_x(0, slot_value(act, BATCH, 0, S - 1))
            raws = [w[:, 1].rearrange("p a k n -> p (a k n)").bitcast(F32) for w in (wi16, wo16)]
            his = [w[:, 0, 0].rearrange("p k n -> p (k n)") for w in (wi16, wo16)]
            drop = z_ps[:].rearrange("p b n -> p (b n)")

            def squares(src, n):
                chain.step(a.activation(drop, src, ACT.Square, accum_out=boot_ss[:, n:n + 1]))
                a.nop().then_inc(s_bsq, 1)

            def hi_parts(m):
                act.wait_ge(s_bscale, (1, 3)[m])
                for q in range(Q):
                    c = slice(q * QN, (q + 1) * QN)
                    a.activation(his[m][:, c], raws[m][:, c], ACT.Copy,
                                 scale=wscale[:, m:m + 1]).then_inc(s_bhi, 1)

            for q in range(Q):
                act.wait_ge(s_braw[q], 16)
                squares(raws[0][:, q * QN:(q + 1) * QN], q)
            act.wait_ge(s_bias[0], 64)
            squares(bi_all[:, 0, :], 2 * Q + 1)
            hi_parts(0)
            for q in range(Q):
                act.wait_ge(s_braw[Q + q], 16)
                squares(raws[1][:, q * QN:(q + 1) * QN], Q + q)
            hi_parts(1)

            pipeline(act, iteration)
            act.wait_ge(s_y, 16 * S)

        @block.vector
        def _(dve):
            v = nc.vector
            chain = Steps(dve, s_dve)
            step = chain.step
            step(v.memset(ones, 1.0))
            dve.wait_ge(s_idx, 64)
            dve.wait_ge(s_iota, 1)

            turns, r = angle[:, 4:6], angle[:, 8:10]
            step(v.tensor_scalar(turns, angle[:, 0:2], 1.0 / 6.283185307179586, TO_INTEGER, ALU.mult, ALU.add))
            step(v.tensor_scalar(turns, turns, -TO_INTEGER, None, ALU.add))
            step(v.tensor_copy(r, angle[:, 0:2]))
            for part in TWO_PI_PARTS:
                step(v.scalar_tensor_tensor(out=r, in0=turns, scalar=-part, in1=r, op0=ALU.mult, op1=ALU.add))
            step(v.tensor_scalar(angle[:, 18:20], r, BELOW_PI, -BELOW_PI, ALU.min, ALU.max))
            step(v.scalar_tensor_tensor(out=r, in0=angle[:, 18:20], scalar=-1.0, in1=angle[:, 18:20],
                                        op0=ALU.mult, op1=ALU.max))
            v.tensor_scalar(angle[:, 16:18], r, -1.0, 1.5707963267948966, ALU.mult, ALU.add).then_inc(s_ang, 1)

            step(v.tensor_copy(keys_e, keys_i))
            step(v.tensor_copy(iota_f, iota_i))
            step(v.tensor_scalar(keys_k, keys_e, 0.0, float(E), ALU.is_lt, ALU.mult))
            step(v.tensor_tensor(keys_e, keys_e, keys_k, ALU.add))
            step(v.tensor_scalar(keys_e, keys_e, 0.0, E - 1.0, ALU.max, ALU.min))
            step(v.scalar_tensor_tensor(out=keys_k, in0=keys_e, scalar=float(S), in1=iota_f, op0=ALU.mult, op1=ALU.add))
            pos, start, first, rank, fe = (cols[:, j:j + 1] for j in range(5))
            e_col, k_col, i_col = keys_e[:, S:S + 1], keys_k[:, S:S + 1], iota_f[:, S:S + 1]
            step(v.tensor_scalar(less, keys_k[:, 0:S], k_col, None, ALU.is_lt))
            step(v.reduce_sum(pos, less, AX.X))
            step(v.tensor_scalar(less, keys_e[:, 0:S], e_col, None, ALU.is_lt))
            step(v.reduce_sum(start, less, AX.X))
            step(v.tensor_tensor(first, pos, start, ALU.is_equal))
            step(v.tensor_tensor(fe, first, e_col, ALU.mult))
            step(v.tensor_scalar(onehot, iota_f[:, 0:S], pos, None, ALU.is_equal))
            v.tensor_scalar(less, keys_e[:, 0:S], e_col, None, ALU.is_gt).then_inc(s_less, 1)
            dve.wait_ge(s_rankp, 1)
            step(v.tensor_copy(rank, xT_ps[:, 0:1]))
            step(v.tensor_scalar(onehot_r, iota_f[:, 0:E], rank, None, ALU.is_equal))
            step(v.tensor_scalar(after_r, iota_f[:, 0:E + 1], rank, None, ALU.is_gt))
            v.engine_nop().then_inc(s_onehot, 1)
            dve.wait_ge(s_tabp, 1)
            v.tensor_copy(tab[0:1, BATCH:BATCH + S], xT_ps[0:1, 0:S])
            v.tensor_copy(tab[0:1, RANK:RANK + S], xT_ps[0:1, S:2 * S])
            v.tensor_copy(tab[0:1, EXPERT:EXPERT + E], xT_ps[0:1, 2 * S:2 * S + E])
            v.tensor_copy(tab[0:1, BEFORE:BEFORE + E + 1], xT_ps[0:1, 3 * S:3 * S + E + 1])
            wrapped, reached = keys_e[0:1, 0:S], keys_k[0:1, 0:S]
            step(v.tensor_copy(wrapped, xT_ps[0:1, S:2 * S]))
            for m in range(RB, E, RB):
                step(v.tensor_scalar(reached, xT_ps[0:1, S:2 * S], float(m), -float(RB), ALU.is_ge, ALU.mult))
                step(v.tensor_tensor(wrapped, wrapped, reached, ALU.add))
            step(v.tensor_copy(tab[0:1, BUF3:BUF3 + S], wrapped))
            step(v.tensor_scalar(tab[0:1, BUF:BUF + S], tab[0:1, RANK:RANK + S], 1, None, ALU.bitwise_and))
            v.engine_nop().then_inc(s_tables, 1)

            dve.wait_ge(s_sin, 1)
            for j in range(4):
                step(v.tensor_copy(spread[:, j * P:(j + 1) * P], angle[:, 20 + j:21 + j].to_broadcast([P, P])))
            v.engine_nop().then_inc(s_onehot, 1)
            dve.wait_ge(s_tabp, 2)
            for col, src, sign in ((0, 0, 1), (1, 0, 1), (2, 1, 1), (3, 1, 1), (4, 2, -1), (5, 2, 1), (6, 3, -1), (7, 3, 1)):
                step(v.tensor_scalar(rot[:, :, col], o_ps[:, src * S:(src + 1) * S], float(sign), None, ALU.mult))

            def row(tile, b, cols=slice(None)):
                return tile[:, bass.ds(b, 1), cols].rearrange("p a n -> p (a n)")

            def as_int(ap):
                return ap.bitcast(I32)

            def scale_x(s, inner):
                dve.wait_ge(s_sq, s + 1)
                if inner or s >= 1:
                    dve.wait_ge(s_xs, s)
                step(v.tensor_scalar(as_int(TM), as_int(SS), 24, None, ALU.logical_shift_right))
                step(v.tensor_scalar(as_int(row(inv, s % XB, slice(ISX, ISX + 1))), as_int(TM),
                                     float(EXP1), float(INVERSE * EXP1), ALU.mult, ALU.add))
                v.tensor_scalar(as_int(SX), as_int(TM), float(-EXP1), float(SCALE * EXP1),
                                ALU.mult, ALU.add).then_inc(s_sx, 1)

            def scale_h(s, b, inner):
                if inner or s >= 1:
                    dve.wait_ge(s_hs, s * NB)
                isx = row(inv, s % XB, slice(ISX, ISX + 1))
                ish = row(inv, s % XB, slice(ISH, ISH + 1))
                of = lambda k: row(ex, b, slice(k, k + 1))
                step(v.tensor_scalar(TB, isx, of(AWI), of(NBI), ALU.mult, ALU.add))
                step(v.tensor_scalar(as_int(TM), as_int(TB), 23, None, ALU.logical_shift_right))
                step(v.tensor_scalar(as_int(SH), as_int(TM), float(-EXP1), float(SCALE_F * EXP1), ALU.mult, ALU.add))
                step(v.tensor_scalar(as_int(ish), as_int(TM), float(EXP1), float(INVERSE_F * EXP1), ALU.mult, ALU.add))
                step(v.tensor_tensor(ZS, isx, of(IWI), ALU.mult))

            def z_bank(s, n, b, inner):
                dve.wait_ge(s_g1, s * NB + n + 1)
                if inner or s >= 1:
                    dve.wait_ge(s_hT, (s - 1) * NB + n + 1)
                hb = slice(n * BANK, (n + 1) * BANK)
                v.scalar_tensor_tensor(out=hid[:, hb], in0=z_ps[:, n, :], scalar=ZS,
                                       in1=row(bi_all, b, hb), op0=ALU.mult, op1=ALU.add).then_inc(s_z, 1)

            def lo_group(s, n):
                dve.wait_ge(s_hhi, (s) * NB + n + 1)
                v.tensor_tensor(hT16[:, n % 2, 1].rearrange("p c t -> p (c t)"), hT_ps[:, n % 2, :],
                                hT16[:, n % 2, 0].rearrange("p c t -> p (c t)"), ALU.subtract).then_inc(s_hlo, 1)

            os, mean, var, t, rstd = ln[:, 0:1], ln[:, 1:2], ln[:, 2:3], ln[:, 3:4], ln[:, 4:5]

            def residual(s, b, inner):
                dve.wait_ge(s_g2, (s + 1) * NB)
                step(v.tensor_tensor(os, row(inv, s % XB, slice(ISH, ISH + 1)), row(ex, b, slice(IWO, IWO + 1)), ALU.mult))
                xr = row(xbuf, s % XB)
                v.scalar_tensor_tensor(out=xr, in0=o_ps[:], scalar=os, in1=xr, op0=ALU.mult, op1=ALU.add).then_inc(s_res, 1)

            def normalise(s, b3):
                bgb = lambda j: bgb_all[:, bass.ds(b3, 1), j, :].rearrange("p a n -> p (a n)")
                xr = row(xbuf, s % XB)
                dve.wait_ge(s_res, s + 1)
                step(v.tensor_tensor(xr, xr, bgb(0), ALU.add))
                step(v.bn_stats(ln[:, 8:14], xr))
                step(v.bn_aggr(ln[:, 1:3], ln[:, 8:14]))
                step(v.tensor_scalar(var, var, LN_EPS, None, ALU.add))
                step(v.tensor_scalar(as_int(t), as_int(var), 1, None, ALU.logical_shift_right))
                step(v.tensor_scalar(as_int(rstd), as_int(t), -1.0, float(0x5F3759DF), ALU.mult, ALU.add))
                for _ in range(3):
                    step(v.scalar_tensor_tensor(out=t, in0=rstd, scalar=var, in1=rstd, op0=ALU.mult, op1=ALU.mult))
                    step(v.tensor_scalar(t, t, -0.5, 1.5, ALU.mult, ALU.add))
                    step(v.tensor_tensor(rstd, rstd, t, ALU.mult))
                step(v.tensor_scalar(xr, xr, mean, rstd, ALU.subtract, ALU.mult))
                step(v.tensor_tensor(xr, xr, bgb(1), ALU.mult))
                v.tensor_tensor(xr, xr, bgb(2), ALU.add).then_inc(s_ln, 1)

            quads = lambda ap: ap.rearrange("p (d f) -> p d f", f=4)
            pairs = lambda ap: ap.rearrange("p (d f) -> p d f", f=2)

            def rotate_products(s, inner):
                table = lambda k: rot[:, bass.ds(s, 1), k:k + 4].to_broadcast([P, H // 4, 4])
                xr = row(xbuf, s % XB)
                dve.wait_ge(s_ln, s + 1)
                step(v.tensor_tensor(quads(turned[:]), quads(xr), table(4), ALU.mult))
                if inner or s >= 1:
                    dve.wait_ge(s_y, s * 16)
                step(v.tensor_tensor(quads(y[:]), quads(xr), table(0), ALU.mult))

            def rotate_sums():
                step(v.tensor_tensor(pairs(y[:])[:, :, 0], pairs(y[:])[:, :, 0], pairs(turned[:])[:, :, 1], ALU.add))
                v.tensor_tensor(pairs(y[:])[:, :, 1], pairs(y[:])[:, :, 1], pairs(turned[:])[:, :, 0], ALU.add).then_inc(s_done, 1)

            def iteration(s, inner=False):
                chain.clear()
                ahead, here = there(s, 1, inner), there(s, 0, inner)
                back, last = there(s, -1, inner), there(s, -2, inner)
                if here:
                    b, r = slot_value(dve, BUF, s, 1), slot_value(dve, RANK, s, E - 1)
                if last:
                    b2, b3 = slot_value(dve, BUF, s - 2, 1), slot_value(dve, BUF3, s - 2, RB - 1)
                    residual(s - 2, b2, inner)
                if here:
                    dve.wait_ge(s_wi, r + 1)
                    scale_h(s, b, inner)
                if ahead:
                    scale_x(s + 1, inner)
                if last:
                    normalise(s - 2, b3)
                if back:
                    lo_group(s - 1, 0)
                if here:
                    z_bank(s, 0, b, inner)
                if last:
                    rotate_products(s - 2, inner)
                if back:
                    lo_group(s - 1, 1)
                if ahead:
                    dve.wait_ge(s_xhi, s + 2)
                    v.tensor_tensor(xT16[:, 1].rearrange("p k t -> p (k t)"), xT_ps[:],
                                    xT16[:, 0].rearrange("p k t -> p (k t)"), ALU.subtract).then_inc(s_xlo, 1)
                if here:
                    z_bank(s, 1, b, inner)
                if last:
                    rotate_sums()
                if back:
                    lo_group(s - 1, 2)
                if here:
                    z_bank(s, 2, b, inner)
                if back:
                    lo_group(s - 1, 3)
                if here:
                    z_bank(s, 3, b, inner)

            raws = [w[:, 1].rearrange("p a k n -> p (a k n)").bitcast(F32) for w in (wi16, wo16)]
            his = [w[:, 0, 0].rearrange("p k n -> p (k n)") for w in (wi16, wo16)]
            los = [w[:, 0, 1].rearrange("p k n -> p (k n)") for w in (wi16, wo16)]

            def total(m):
                step(v.reduce_sum(boot_ss[:, 2 * Q + 2 * m:2 * Q + 2 * m + 1], boot_ss[:, m * Q:(m + 1) * Q], AX.X))
                v.engine_nop().then_inc(s_bsum, 1)

            def lo_parts(m):
                for q in range(Q):
                    c = slice(q * QN, (q + 1) * QN)
                    dve.wait_ge(s_bhi, m * Q + q + 1)
                    step(v.scalar_tensor_tensor(out=los[m][:, c], in0=raws[m][:, c], scalar=wscale[:, m:m + 1],
                                                in1=his[m][:, c], op0=ALU.mult, op1=ALU.subtract))
                v.engine_nop().then_inc((s_wi, s_wo)[m], 1)

            dve.wait_ge(s_bsq, Q)
            total(0)
            dve.wait_ge(s_bsq, Q + 1)
            v.engine_nop().then_inc(s_bsum, 1)
            dve.wait_ge(s_bscale, 2)
            lo_parts(0)
            dve.wait_ge(s_bsq, 2 * Q + 1)
            total(1)
            dve.wait_ge(s_bscale, 3)
            lo_parts(1)

            pipeline(dve, iteration)

        @block.tensor
        def _(pe):
            t = nc.tensor
            fe, first, rank = cols[:, 4:5], cols[:, 2:3], cols[:, 3:4]
            pe.wait_ge(s_less, 1)
            t.matmul(xT_ps[:, 0:1], less, first, start=True, stop=True).then_inc(s_rankp, 1)
            pe.wait_ge(s_onehot, 1)
            t.matmul(xT_ps[0:1, 0:S], iota_f[:, S:S + 1], onehot, start=True, stop=True)
            t.matmul(xT_ps[0:1, S:2 * S], rank, onehot, start=True, stop=True)
            t.matmul(xT_ps[0:1, 2 * S:2 * S + E], fe, onehot_r, start=True, stop=True)
            t.matmul(xT_ps[0:1, 3 * S:3 * S + E + 1], ones, after_r, start=True, stop=True).then_inc(s_tabp, 1)
            pe.wait_ge(s_onehot, 2)
            for j in range(4):
                last = t.matmul(o_ps[:, j * S:(j + 1) * S], spread[:, j * P:(j + 1) * P], onehot, start=True, stop=True)
            last.then_inc(s_tabp, 1)
            pe.wait_ge(s_tables, 1)
            pe.wait_ge(s_ident, 1)

            PASSES = ((1, 0), (0, 1), (0, 0))

            def transpose_h(s, n, inner):
                G = s * NB + n
                pe.wait_ge(s_hs, G + 1)
                if inner or G >= 2:
                    pe.wait_ge(s_hlo, G - 1)
                for c in range(GC):
                    last = t.transpose(hT_ps[:, n % 2, c * P:(c + 1) * P],
                                       hid[:, (n * GC + c) * P:(n * GC + c + 1) * P], ident[:])
                last.then_inc(s_hT, 1)

            def first_product(s, n, b, inner):
                if inner or s >= 1:
                    pe.wait_ge(s_z, (s - 1) * NB + n + 1)
                cs = slice(n * BANK, (n + 1) * BANK)
                for k in range(KH):
                    for a, w in PASSES:
                        last = t.matmul(z_ps[:, n, :], xT16[:, a, k, :], wi16[:, bass.ds(b, 1), w, k, cs],
                                        start=(k == 0 and (a, w) == PASSES[0]),
                                        stop=(k == KH - 1 and (a, w) == PASSES[-1]))
                last.then_inc(s_g1, 1)

            def second_product(s, n, b):
                pe.wait_ge(s_hlo, s * NB + n + 1)
                for c in range(GC):
                    for a, w in PASSES:
                        last = t.matmul(o_ps[:], hT16[:, n % 2, a, c, :], wo16[:, bass.ds(b, 1), w, n * GC + c, :],
                                        start=(n == 0 and c == 0 and (a, w) == PASSES[0]),
                                        stop=(n == NB - 1 and c == GC - 1 and (a, w) == PASSES[-1]))
                last.then_inc(s_g2, 1)

            def iteration(s, inner=False):
                if there(s, -2, inner):
                    second_product(s - 2, NB - 1, slot_value(pe, BUF, s - 2, 1))
                if there(s, 0, inner):
                    b, r = slot_value(pe, BUF, s, 1), slot_value(pe, RANK, s, E - 1)
                if there(s, 0, inner):
                    pe.wait_ge(s_wi, r + 1)
                    pe.wait_ge(s_xlo, s + 1)
                    for n in range(NB - 1):
                        first_product(s, n, b, inner)
                if there(s, -1, inner):
                    transpose_h(s - 1, 0, inner)
                if there(s, 0, inner):
                    first_product(s, NB - 1, b, inner)
                if there(s, -1, inner):
                    transpose_h(s - 1, 1, inner)
                if there(s, 1, inner):
                    pe.wait_ge(s_xs, s + 2)
                    for k in range(KH):
                        last = t.transpose(xT_ps[:, k * P:(k + 1) * P], xs[:, k * P:(k + 1) * P], ident[:])
                    last.then_inc(s_xT, 1)
                if there(s, -1, inner):
                    b1 = slot_value(pe, BUF, s - 1, 1)
                    pe.wait_ge(s_wo, slot_value(pe, RANK, s - 1, E - 1) + 1)
                    if inner or s >= 2:
                        pe.wait_ge(s_res, s - 1)
                    second_product(s - 1, 0, b1)
                    transpose_h(s - 1, 2, inner)
                    second_product(s - 1, 1, b1)
                    transpose_h(s - 1, 3, inner)
                    second_product(s - 1, 2, b1)

            pipeline(pe, iteration)


_INS = ["x", "itok_B_0_7", "condB_theta", "condB_phi", "L0_cond_Wi", "L0_cond_bi", "L0_cond_Wo",
        "L0_cond_bo", "L0_cond_gamma", "L0_cond_beta"]


def kernel(**inputs):
    import numpy as np
    import concourse.bacc as bacc
    from concourse import mybir as mb
    from concourse.bass_utils import run_bass_kernel_spmd

    nc = bacc.Bacc("TRN2", target_bir_lowering=False, num_devices=1,
                   dynamic_dma_scratch_size=1024)
    arrays, args = {}, []
    for name in _INS:
        a = np.ascontiguousarray(inputs[name])
        arrays[f"in_{name}"] = a
        args.append(nc.dram_tensor(f"in_{name}", a.shape, mb.dt.from_np(a.dtype), kind="ExternalInput").ap())
    shape = arrays["in_x"].shape
    args.append(nc.dram_tensor("out", shape, mb.dt.float32, kind="ExternalOutput").ap())
    expert_mlp_rotate_kernel(nc, *args)
    result = run_bass_kernel_spmd(nc, [arrays], core_ids=[0])
    return result.results[0]["out"]
```

```python
import concourse.bass as bass
from concourse import mybir
from contextlib import ExitStack

F32 = mybir.dt.float32
F16 = mybir.dt.float16
I32 = mybir.dt.int32
ALU = mybir.AluOpType
ACT = mybir.ActivationFunctionType
AX = mybir.AxisListType
ADD_LANES = bass.bass_isa.ReduceOp.add

P = 128
BANK = 512
LN_EPS = 1e-12
EXP1 = 1 << 23
EXP2 = 1 << 24
SCALE, INVERSE, BOUND = 204, 50, 65
SCALE_F, INVERSE_F = 268, -14
TWO_PI_PARTS = (6.28125, 0.0019350051879882812, 3.0199159819567e-07)
TO_INTEGER = 1.5 * 2.0 ** 23
BELOW_PI = 3.1415925


class Steps:

    def __init__(self, engine, sem):
        self.engine, self.sem, self.n = engine, sem, 0

    def step(self, ins):
        ins.then_inc(self.sem, 1)
        self.n += 1
        self.engine.wait_ge(self.sem, self.n)

    def clear(self):
        self.engine.sem_clear(self.sem)
        self.n = 0


def expert_mlp_rotate_kernel(nc, x, itok, theta, phi, Wi, bi, Wo, bo, gamma, beta, out):
    S, T, H = x.shape
    E, _, I = Wi.shape
    KH, KI = H // P, I // P
    NB = I // BANK
    GC = KI // NB
    Q = 4
    QN = H * I // P // Q
    XB = 8
    RB = 3
    WO_SPLIT = 2
    assert T == P and S == P and H == BANK and E % 2 == 0 and NB == Q == KH

    ctx = ExitStack()
    with ctx:
        def sb(name, shape, dt=F32):
            return ctx.enter_context(nc.sbuf_tensor(name, shape, dt))

        def pb(name, shape, dt=F32):
            return ctx.enter_context(nc.psum_tensor(name, shape, dt))

        def sem(name):
            return ctx.enter_context(nc.semaphore(name))

        wi16 = sb("wi16", [P, 2, 2, KH, I], F16)
        wo16 = sb("wo16", [P, 2, 2, KI, H], F16)
        staged = sb("staged", [P, 2, QN])
        bi_all = sb("bi_all", [P, 2, I])
        bgb_all = sb("bgb_all", [P, RB, 3, H])
        hid = sb("hid", [P, I])
        hT16 = sb("hT16", [P, 2, 2, GC, P], F16)
        xbuf = sb("xbuf", [P, XB, H])
        xs = sb("xs", [P, H])
        xT16 = sb("xT16", [P, 2, KH, P], F16)
        y = sb("y", [P, H])
        turned = sb("turned", [P, H])
        rot = sb("rot", [P, S, 8])
        ident = sb("ident", [P, P])
        tab = sb("tab", [1, 4 * S + 2 * E + 1], I32)
        BATCH, RANK, BUF, BUF3, EXPERT, BEFORE = 0, S, 2 * S, 3 * S, 4 * S, 4 * S + E
        tok = sb("tok", [P, 6])
        SS, SX, SH, ZS, TM, TB = (tok[:, j:j + 1] for j in range(6))
        inv = sb("inv", [P, XB, 2])
        ISX, ISH = range(2)
        ex = sb("ex", [P, 2, 4])
        IWI, AWI, NBI, IWO = range(4)
        wscale = sb("wscale", [P, 2])
        ln = sb("ln", [P, 16])
        consts = sb("consts", [P, 6], I32)
        pool_s = sb("pool_s", [P, 4])
        boot_ss = sb("boot_ss", [P, 2 * Q + 2])

        z_ps = pb("z_ps", [P, NB, BANK])
        hT_ps = pb("hT_ps", [P, 2, BANK])
        xT_ps = pb("xT_ps", [P, BANK])
        o_ps = pb("o_ps", [P, BANK])

        keys_i = hid[:, 0:129].bitcast(I32)
        iota_i = hid[:, 132:261].bitcast(I32)
        keys_e = hid[:, 264:393]
        keys_k = hid[:, 396:525]
        iota_f = hid[:, 528:657]
        less = hid[:, 660:788]
        onehot = hid[:, 792:920]
        onehot_r = hid[:, 924:924 + E]
        after_r = hid[:, 940:940 + E + 1]
        ones = hid[:, 960:961]
        cols = hid[:, 964:980]
        angle = hid[:, 980:1010]
        spread = hid[:, 1024:1024 + 4 * P]

        s_idx = sem("s_idx")
        s_angin = sem("s_angin")
        s_iota = sem("s_iota")
        s_ident = sem("s_ident")
        s_pool = sem("s_pool")
        s_dve = sem("s_dve")
        s_act = sem("s_act")
        s_ang = sem("s_ang")
        s_sin = sem("s_sin")
        s_less = sem("s_less")
        s_rankp = sem("s_rankp")
        s_onehot = sem("s_onehot")
        s_tabp = sem("s_tabp")
        s_tables = sem("s_tables")
        s_braw = [sem(f"s_braw{i}") for i in range(2 * Q)]
        s_bsq = sem("s_bsq")
        s_bsqp = sem("s_bsqp")
        s_bsum = sem("s_bsum")
        s_bscale = sem("s_bscale")
        s_bhi = sem("s_bhi")
        s_blo = sem("s_blo")
        s_bpool = sem("s_bpool")
        s_bias = [sem(f"s_bias{i}") for i in range(2)]
        s_stage = [sem(f"s_stage{i}") for i in range(2)]
        s_unstage = [sem(f"s_unstage{i}") for i in range(2)]
        s_wi = sem("s_wi")
        s_wo = sem("s_wo")
        s_x = sem("s_x")
        s_y = sem("s_y")
        s_sq = sem("s_sq")
        s_sx = sem("s_sx")
        s_xs = sem("s_xs")
        s_xT = sem("s_xT")
        s_xhi = sem("s_xhi")
        s_xlo = sem("s_xlo")
        s_g1 = sem("s_g1")
        s_z = sem("s_z")
        s_gelu = sem("s_gelu")
        s_hs = sem("s_hs")
        s_hT = sem("s_hT")
        s_hhi = sem("s_hhi")
        s_hlo = sem("s_hlo")
        s_g2 = sem("s_g2")
        s_res = sem("s_res")
        s_ln = sem("s_ln")
        s_done = sem("s_done")

        block = ctx.enter_context(nc.Block())

        def slot_value(engine, table, s, top, least=0):
            return engine.value_load(tab[0:1, bass.ds(s + table, 1)], min_val=least, max_val=top)

        def pipeline(engine, iteration):
            iteration(1)
            iteration(2)
            with engine.Fori(3, S - 2) as s:
                iteration(s, True)
            for s in range(S - 2, S + 2):
                iteration(s)

        def there(s, d, inner):
            return inner or 0 <= s + d < S

        @block.sync
        def _(sp):
            sp.dma_start(keys_i[:, 0:S], itok.partition_broadcast(P)).then_inc(s_idx, 16)
            sp.dma_start(keys_i[:, S:S + 1], itok.rearrange("(p o) -> p o", o=1)).then_inc(s_idx, 16)
            sp.dma_start(angle[:, 0:1], theta.rearrange("(p o) -> p o", o=1)).then_inc(s_angin, 16)
            sp.dma_start(angle[:, 1:2], phi.rearrange("(p o) -> p o", o=1)).then_inc(s_angin, 16)

            def weight_quarter(m, e, q):
                if m == 0:
                    return Wi[bass.ds(e, 1), q * P:(q + 1) * P, :].rearrange("e p n -> p (e n)")
                rows = slice(q * GC * P, (q + 1) * GC * P)
                return Wo[bass.ds(e, 1), rows, :].rearrange("e (c p) n -> p (e c) n", p=P)

            def quarter_view(region, m):
                return region if m == 0 else region.rearrange("p (c n) -> p c n", n=H)

            def load_biases(e, b, b3):
                sp.dma_start(bi_all[:, b, :], bi[bass.ds(e, 1), :].broadcast_to([P, I])).then_inc(s_bias[b], 16)
                for j, v in enumerate((bo, gamma, beta)):
                    sp.dma_start(bgb_all[:, b3, j, :], v[bass.ds(e, 1), :].broadcast_to([P, H])).then_inc(s_bias[b], 16)

            sp.wait_ge(s_tables, 1)
            e0 = slot_value(sp, EXPERT, 0, E - 1)
            for m, w in enumerate((wi16, wo16)):
                raw = w[:, 1].rearrange("p a k n -> p (a k n)").bitcast(F32)
                for q in range(Q):
                    sp.dma_start(quarter_view(raw[:, q * QN:(q + 1) * QN], m),
                                 weight_quarter(m, e0, q)).then_inc(s_braw[m * Q + q], 16)
                if m == 0:
                    sp.wait_ge(s_tables, 2)
                    load_biases(e0, 0, 0)

            def rank(r, b, nth):
                e = slot_value(sp, EXPERT, r, E - 1)
                if isinstance(r, int) and r == 1:
                    load_biases(e, b, r)
                else:
                    multiplied, ended = slot_value(sp, BEFORE, r - 1, S, 1), slot_value(sp, BEFORE, r - 2, S)
                    sp.wait_ge(s_res, ended + 1)
                    sp.wait_ge(s_res, multiplied)
                    load_biases(e, b, bass.ds(r % RB, 1))
                j = 0
                for m in range(2):
                    for again in range(2):
                        for q in range(Q):
                            used = (r - 1) * (2 * Q) + j // 2
                            if not isinstance(used, int) or used > 0:
                                sp.wait_ge(s_unstage[j % 2], used)
                            sp.dma_start(quarter_view(staged[:, j % 2, :], m),
                                         weight_quarter(m, e, q)).then_inc(s_stage[j % 2], 16)
                            j += 1

            rank(1, 1, 0)
            with sp.Fori(1, E // 2) as i:
                rank(i * 2, 0, i)
                rank(i * 2 + 1, 1, i)

        @block.gpsimd
        def _(pool):
            g = nc.gpsimd
            chain = Steps(pool, s_pool)
            g.iota(iota_i[:, 0:S], [[1, S]], base=0, channel_multiplier=0)
            g.iota(iota_i[:, S:S + 1], [[1, 1]], base=0, channel_multiplier=1)
            for j, c in enumerate((EXP2, EXP1, SCALE * EXP1, INVERSE * EXP1, (INVERSE + 30) * EXP1,
                                   BOUND * EXP1)):
                last = g.memset(consts[:, j:j + 1], c)
            last.then_inc(s_iota, 1)
            chain.step(g.memset(ident[:], 0.0))
            g.affine_select(out=ident[:], in_=ident[:], compare_op=ALU.not_equal, fill=1.0, base=0,
                            pattern=[[-1, P]], channel_multiplier=1).then_inc(s_ident, 1)

            def scale_of(ss, scale_out, outs, chain):
                c = consts
                chain.step(g.tensor_tensor(pool_s[:, 1:2].bitcast(I32), ss.bitcast(I32), c[:, 0:1], ALU.divide))
                chain.step(g.tensor_tensor(pool_s[:, 2:3].bitcast(I32), pool_s[:, 1:2].bitcast(I32), c[:, 1:2], ALU.mult))
                t = pool_s[:, 2:3].bitcast(I32)
                if scale_out is not None:
                    chain.step(g.tensor_tensor(scale_out.bitcast(I32), c[:, 2:3], t, ALU.subtract))
                for o, j in outs:
                    chain.step(g.tensor_tensor(o.bitcast(I32), t, c[:, j:j + 1], ALU.add))

            def scales(what, ss, b, chain):
                col = lambda k: ex[:, b, k:k + 1]
                if what == "wi":
                    scale_of(ss, wscale[:, 0:1], [(col(IWI), 3), (col(AWI), 4)], chain)
                elif what == "wo":
                    scale_of(ss, wscale[:, 1:2], [(col(IWO), 3)], chain)
                else:
                    scale_of(ss, None, [(col(NBI), 5)], chain)

            def boot_matrix(m):
                pool.wait_ge(s_bsum, m + 1)
                chain.step(g.partition_all_reduce(pool_s[:, 0:1], boot_ss[:, 2 * Q + m:2 * Q + m + 1], P, ADD_LANES))
                scales(("wi", "wo")[m], pool_s[:, 0:1], 0, chain)
                g.engine_nop().then_inc(s_bscale, 1)

            def boot_bias():
                pool.wait_ge(s_bias[0], 64)
                for n in range(NB):
                    piece = bi_all[:, 0, n * BANK:(n + 1) * BANK]
                    chain.step(g.tensor_tensor((y if n else turned)[:], piece, piece, ALU.mult))
                    if n:
                        chain.step(g.tensor_tensor(turned[:], turned[:], y[:], ALU.add))
                w = BANK // 2
                while w:
                    chain.step(g.tensor_tensor(turned[:, 0:w], turned[:, 0:w], turned[:, w:2 * w], ALU.add))
                    w //= 2
                scales("bi", turned[:, 0:1], 0, chain)
                g.engine_nop().then_inc(s_bscale, 1)

            PIECE = 512

            def fold(acc):
                w = QN // 2
                while w:
                    chain.step(g.tensor_tensor(acc[:, 0:w], acc[:, 0:w], acc[:, w:2 * w], ALU.add))
                    w //= 2
                return acc[:, 0:1]

            def split(hi, lo, raw, scale):
                chain.step(g.tensor_scalar(hi, raw, scale, 1.0, ALU.mult, ALU.mult))
                chain.step(g.tensor_scalar(raw, raw, scale, 1.0, ALU.mult, ALU.mult))
                chain.step(g.tensor_tensor(lo, raw, hi, ALU.subtract))

            flat = lambda w, b: w[:, b].rearrange("p a k n -> p (a k n)")
            acc0 = flat(wo16, 0).bitcast(F32)[:, Q * QN // 2:Q * QN // 2 + QN]
            first_raw = flat(wi16, 1).bitcast(F32)[:, 0:QN]
            pool.wait_ge(s_braw[0], 16)
            chain.step(g.tensor_tensor(acc0, first_raw, first_raw, ALU.mult))
            chain.step(g.tensor_copy(boot_ss[:, 0:1], fold(acc0)))
            g.engine_nop().then_inc(s_bsqp, 1)
            boot_matrix(0)
            boot_bias()
            boot_matrix(1)
            for q in range(WO_SPLIT, Q):
                pool.wait_ge(s_braw[Q + q], 16)
                for at in range(q * QN, (q + 1) * QN, PIECE):
                    p = slice(at, at + PIECE)
                    split(flat(wo16, 0)[:, p], flat(wo16, 0)[:, Q * QN + at:Q * QN + at + PIECE],
                          flat(wo16, 1).bitcast(F32)[:, p], wscale[:, 1:2])
                g.engine_nop().then_inc(s_bpool, 1)
            pool.wait_ge(s_blo, Q + WO_SPLIT)
            g.engine_nop().then_inc(s_wo, 1)

            def rank(r, b, nth):
                chain.clear()
                boot = isinstance(r, int) and r == 1
                before = None if boot else slot_value(pool, BEFORE, r - 1, S, 1)

                def quarter(j):
                    pool.wait_ge(s_stage[j % 2], 16)
                    pool.sem_clear(s_stage[j % 2])
                    return staged[:, j % 2, :]

                j = 0
                for m, w in enumerate((wi16, wo16)):
                    hi = w[:, b, 0].rearrange("p k n -> p (k n)")
                    lo = w[:, b, 1].rearrange("p k n -> p (k n)")
                    room = lo.bitcast(F32)
                    acc, sq = room[:, 0:QN], room[:, QN:2 * QN]
                    for q in range(Q):
                        raw = quarter(j)
                        if j == 0 and not boot:
                            pool.wait_ge(s_res, before)
                        for at in range(0, QN, PIECE):
                            p = slice(at, at + PIECE)
                            to = (acc if q == 0 else sq)[:, p]
                            chain.step(g.tensor_tensor(to, raw[:, p], raw[:, p], ALU.mult))
                            if q:
                                chain.step(g.tensor_tensor(acc[:, p], acc[:, p], sq[:, p], ALU.add))
                        g.engine_nop().then_inc(s_unstage[j % 2], 1)
                        j += 1
                    fold(acc)
                    chain.step(g.partition_all_reduce(pool_s[:, 0:1], acc[:, 0:1], P, ADD_LANES))
                    scales(("wi", "wo")[m], pool_s[:, 0:1], b, chain)
                    if m == 0:
                        pool.wait_ge(s_bias[b], nth * 64 + 64)
                        chain.step(g.tensor_tensor(acc, bi_all[:, b, :], bi_all[:, b, :], ALU.mult))
                        fold(acc)
                        scales("bi", acc[:, 0:1], b, chain)
                    for q in range(Q):
                        raw = quarter(j)
                        for at in range(0, QN, PIECE):
                            p, o = slice(at, at + PIECE), slice(q * QN + at, q * QN + at + PIECE)
                            split(hi[:, o], lo[:, o], raw[:, p], wscale[:, m:m + 1])
                        g.engine_nop().then_inc(s_unstage[j % 2], 1)
                        j += 1
                    g.engine_nop().then_inc((s_wi, s_wo)[m], 1)

            rank(1, 1, 0)
            with pool.Fori(1, E // 2) as i:
                rank(i * 2, 0, i)
                rank(i * 2 + 1, 1, i)

        @block.scalar
        def _(act):
            a = nc.scalar
            chain = Steps(act, s_act)

            def load_x(s, b):
                act.dma_start(xbuf[:, bass.ds(s % XB, 1), :].rearrange("p a n -> p (a n)"),
                              x[bass.ds(b, 1), :, :].rearrange("a t n -> t (a n)")).then_inc(s_x, 16)

            def x_of(s):
                return xbuf[:, bass.ds(s % XB, 1), :].rearrange("p a n -> p (a n)")

            def sum_x(s, inner=False):
                if there(s, 2, inner):
                    b = slot_value(act, BATCH, s + 2, S - 1)
                if there(s, 1, inner):
                    act.wait_ge(s_x, (s + 2) * 16)
                    if inner or s >= 0:
                        act.wait_ge(s_xT, s + 1)
                if there(s, 2, inner):
                    if inner or s >= 3:
                        act.wait_ge(s_done, s - 2)
                    load_x(s + 2, b)
                if there(s, 1, inner):
                    a.activation(xs[:], x_of(s + 1), ACT.Square, accum_out=SS).then_inc(s_sq, 1)

            def scaled_x(s, inner=False):
                if there(s, 1, inner):
                    act.wait_ge(s_sx, 1)
                    act.sem_clear(s_sx)
                    a.activation(xs[:], x_of(s + 1), ACT.Copy, scale=SX).then_inc(s_xs, 1)

            def hi_x(s, inner=False):
                if there(s, 1, inner):
                    act.wait_ge(s_xT, s + 2)
                    a.activation(xT16[:, 0].rearrange("p k t -> p (k t)"), xT_ps[:],
                                 ACT.Copy).then_inc(s_xhi, 1)

            def iteration(s, inner=False):
                x_here = inner or s > 0
                if x_here:
                    sum_x(s, inner)
                    scaled_x(s, inner)

                def hi_group(n):
                    G = (s - 1) * NB + n
                    act.wait_ge(s_hT, G + 1)
                    if inner or G >= 2:
                        act.wait_ge(s_g2, G - 1)
                    a.activation(hT16[:, n % 2, 0].rearrange("p c t -> p (c t)"), hT_ps[:, n % 2, :],
                                 ACT.Copy).then_inc(s_hhi, 1)

                def gelu_bank(n):
                    hb = hid[:, n * BANK:(n + 1) * BANK]
                    act.wait_ge(s_z, s * NB + n + 1)
                    a.activation(hb, hb, ACT.Gelu).then_inc(s_gelu, 1)
                    act.wait_ge(s_gelu, s * NB + n + 1)
                    a.activation(hb, hb, ACT.Copy, scale=SH).then_inc(s_hs, 1)

                back, here = there(s, -1, inner), there(s, 0, inner)
                if back:
                    hi_group(0)
                    hi_group(1)
                if x_here:
                    hi_x(s, inner)
                if here:
                    gelu_bank(0)
                if back:
                    hi_group(2)
                if here:
                    gelu_bank(1)
                if back:
                    hi_group(3)
                if here:
                    gelu_bank(2)
                    gelu_bank(3)
                if there(s, -2, inner):
                    b = slot_value(act, BATCH, s - 2, S - 1)
                    act.wait_ge(s_done, s - 1)
                    act.dma_start(out[bass.ds(b, 1), :, :].rearrange("a t n -> t (a n)"),
                                  y[:]).then_inc(s_y, 16)

            raws = [w[:, 1].rearrange("p a k n -> p (a k n)").bitcast(F32) for w in (wi16, wo16)]
            his = [w[:, 0, 0].rearrange("p k n -> p (k n)") for w in (wi16, wo16)]
            drop = his[1].bitcast(F32)[:, 0:QN]

            def squares(m, q):
                act.wait_ge(s_braw[m * Q + q], 16)
                n = m * Q + q
                chain.step(a.activation(drop, raws[m][:, q * QN:(q + 1) * QN], ACT.Square,
                                        accum_out=boot_ss[:, n:n + 1]))
                a.nop().then_inc(s_bsq, 1)

            def hi_parts(m):
                act.wait_ge(s_bscale, (1, 3)[m])
                for q in range((Q, WO_SPLIT)[m]):
                    c = slice(q * QN, (q + 1) * QN)
                    a.activation(his[m][:, c], raws[m][:, c], ACT.Copy,
                                 scale=wscale[:, m:m + 1]).then_inc(s_bhi, 1)

            act.wait_ge(s_tables, 1)
            load_x(0, slot_value(act, BATCH, 0, S - 1))
            act.wait_ge(s_tables, 2)
            sum_x(-1)
            squares(0, 1)
            scaled_x(-1)
            squares(0, 2)
            hi_x(-1)
            squares(0, 3)
            act.wait_ge(s_ang, 1)
            a.activation(angle[:, 20:24], angle[:, 16:20], ACT.Sin).then_inc(s_sin, 1)
            sum_x(0)
            hi_parts(0)
            scaled_x(0)
            for q in range(Q):
                squares(1, q)
            hi_x(0)
            hi_parts(1)
            iteration(0)

            pipeline(act, iteration)
            act.wait_ge(s_y, 16 * S)

        @block.vector
        def _(dve):
            v = nc.vector
            chain = Steps(dve, s_dve)
            step = chain.step
            step(v.memset(ones, 1.0))
            dve.wait_ge(s_idx, 32)
            dve.wait_ge(s_iota, 1)

            step(v.tensor_copy(keys_e, keys_i))
            step(v.tensor_copy(iota_f, iota_i))
            step(v.tensor_scalar(keys_k, keys_e, 0.0, float(E), ALU.is_lt, ALU.mult))
            step(v.tensor_tensor(keys_e, keys_e, keys_k, ALU.add))
            step(v.tensor_scalar(keys_e, keys_e, 0.0, E - 1.0, ALU.max, ALU.min))
            step(v.scalar_tensor_tensor(out=keys_k, in0=keys_e, scalar=float(S), in1=iota_f, op0=ALU.mult, op1=ALU.add))
            least = cols[0:1, 5:7].bitcast(I32)
            step(v.tensor_reduce(cols[0:1, 5:6], keys_k[0:1, 0:S], AX.X, ALU.min))
            step(v.tensor_copy(least[:, 1:2], cols[0:1, 5:6]))
            step(v.tensor_scalar(tab[0:1, EXPERT:EXPERT + 1], least[:, 1:2], S.bit_length() - 1, None, ALU.logical_shift_right))
            v.tensor_scalar(tab[0:1, BATCH:BATCH + 1], least[:, 1:2], S - 1, None, ALU.bitwise_and).then_inc(s_tables, 1)
            pos, start, first, rank, fe = (cols[:, j:j + 1] for j in range(5))
            e_col, k_col, i_col = keys_e[:, S:S + 1], keys_k[:, S:S + 1], iota_f[:, S:S + 1]
            step(v.tensor_scalar(less, keys_k[:, 0:S], k_col, None, ALU.is_lt))
            step(v.reduce_sum(pos, less, AX.X))
            step(v.tensor_scalar(less, keys_e[:, 0:S], e_col, None, ALU.is_lt))
            step(v.reduce_sum(start, less, AX.X))
            step(v.tensor_tensor(first, pos, start, ALU.is_equal))
            step(v.tensor_tensor(fe, first, e_col, ALU.mult))
            step(v.tensor_scalar(onehot, iota_f[:, 0:S], pos, None, ALU.is_equal))
            v.tensor_scalar(less, keys_e[:, 0:S], e_col, None, ALU.is_gt).then_inc(s_less, 1)
            dve.wait_ge(s_rankp, 1)
            step(v.tensor_copy(rank, xT_ps[:, 0:1]))
            step(v.tensor_scalar(onehot_r, iota_f[:, 0:E], rank, None, ALU.is_equal))
            step(v.tensor_scalar(after_r, iota_f[:, 0:E + 1], rank, None, ALU.is_gt))
            v.engine_nop().then_inc(s_onehot, 1)
            dve.wait_ge(s_tabp, 1)
            v.tensor_copy(tab[0:1, BATCH + 1:BATCH + S], xT_ps[0:1, 1:S])
            v.tensor_copy(tab[0:1, RANK:RANK + S], xT_ps[0:1, S:2 * S])
            v.tensor_copy(tab[0:1, EXPERT + 1:EXPERT + E], xT_ps[0:1, 2 * S + 1:2 * S + E])
            v.tensor_copy(tab[0:1, BEFORE:BEFORE + E + 1], xT_ps[0:1, 3 * S:3 * S + E + 1])
            wrapped, reached = keys_e[0:1, 0:S], keys_k[0:1, 0:S]
            step(v.tensor_copy(wrapped, xT_ps[0:1, S:2 * S]))
            for m in range(RB, E, RB):
                step(v.tensor_scalar(reached, xT_ps[0:1, S:2 * S], float(m), -float(RB), ALU.is_ge, ALU.mult))
                step(v.tensor_tensor(wrapped, wrapped, reached, ALU.add))
            step(v.tensor_copy(tab[0:1, BUF3:BUF3 + S], wrapped))
            step(v.tensor_scalar(tab[0:1, BUF:BUF + S], tab[0:1, RANK:RANK + S], 1, None, ALU.bitwise_and))
            v.engine_nop().then_inc(s_tables, 1)

            def row(tile, b, cols=slice(None)):
                return tile[:, bass.ds(b, 1), cols].rearrange("p a n -> p (a n)")

            def as_int(ap):
                return ap.bitcast(I32)

            def scale_x(s, inner):
                dve.wait_ge(s_sq, s + 1)
                if inner or s >= 1:
                    dve.wait_ge(s_xs, s)
                step(v.tensor_scalar(as_int(TM), as_int(SS), 24, None, ALU.logical_shift_right))
                step(v.tensor_scalar(as_int(row(inv, s % XB, slice(ISX, ISX + 1))), as_int(TM),
                                     float(EXP1), float(INVERSE * EXP1), ALU.mult, ALU.add))
                v.tensor_scalar(as_int(SX), as_int(TM), float(-EXP1), float(SCALE * EXP1),
                                ALU.mult, ALU.add).then_inc(s_sx, 1)

            def scale_h(s, b, inner):
                if inner or s >= 1:
                    dve.wait_ge(s_hs, s * NB)
                isx = row(inv, s % XB, slice(ISX, ISX + 1))
                ish = row(inv, s % XB, slice(ISH, ISH + 1))
                of = lambda k: row(ex, b, slice(k, k + 1))
                step(v.tensor_scalar(TB, isx, of(AWI), of(NBI), ALU.mult, ALU.add))
                step(v.tensor_scalar(as_int(TM), as_int(TB), 23, None, ALU.logical_shift_right))
                step(v.tensor_scalar(as_int(SH), as_int(TM), float(-EXP1), float(SCALE_F * EXP1), ALU.mult, ALU.add))
                step(v.tensor_scalar(as_int(ish), as_int(TM), float(EXP1), float(INVERSE_F * EXP1), ALU.mult, ALU.add))
                step(v.tensor_scalar(ZS, isx, of(IWI), None, ALU.mult))

            def z_bank(s, n, b, inner):
                dve.wait_ge(s_g1, s * NB + n + 1)
                if inner or s >= 1:
                    dve.wait_ge(s_hT, (s - 1) * NB + n + 1)
                hb = slice(n * BANK, (n + 1) * BANK)
                v.scalar_tensor_tensor(out=hid[:, hb], in0=z_ps[:, n, :], scalar=ZS,
                                       in1=row(bi_all, b, hb), op0=ALU.mult, op1=ALU.add).then_inc(s_z, 1)

            def lo_x(s):
                dve.wait_ge(s_xhi, s + 1)
                v.tensor_tensor(xT16[:, 1].rearrange("p k t -> p (k t)"), xT_ps[:],
                                xT16[:, 0].rearrange("p k t -> p (k t)"), ALU.subtract).then_inc(s_xlo, 1)

            def lo_group(s, n):
                dve.wait_ge(s_hhi, (s) * NB + n + 1)
                v.tensor_tensor(hT16[:, n % 2, 1].rearrange("p c t -> p (c t)"), hT_ps[:, n % 2, :],
                                hT16[:, n % 2, 0].rearrange("p c t -> p (c t)"), ALU.subtract).then_inc(s_hlo, 1)

            os, mean, var, t, rstd = ln[:, 0:1], ln[:, 1:2], ln[:, 2:3], ln[:, 3:4], ln[:, 4:5]

            def residual(s, b, inner):
                dve.wait_ge(s_g2, (s + 1) * NB)
                step(v.tensor_scalar(os, row(inv, s % XB, slice(ISH, ISH + 1)), row(ex, b, slice(IWO, IWO + 1)), None, ALU.mult))
                xr = row(xbuf, s % XB)
                v.scalar_tensor_tensor(out=xr, in0=o_ps[:], scalar=os, in1=xr, op0=ALU.mult, op1=ALU.add).then_inc(s_res, 1)

            def normalise(s, b3):
                bgb = lambda j: bgb_all[:, bass.ds(b3, 1), j, :].rearrange("p a n -> p (a n)")
                xr = row(xbuf, s % XB)
                dve.wait_ge(s_res, s + 1)
                step(v.tensor_tensor(xr, xr, bgb(0), ALU.add))
                step(v.bn_stats(ln[:, 8:14], xr))
                step(v.bn_aggr(ln[:, 1:3], ln[:, 8:14]))
                step(v.tensor_scalar(var, var, LN_EPS, None, ALU.add))
                step(v.tensor_scalar(as_int(t), as_int(var), 1, None, ALU.logical_shift_right))
                step(v.tensor_scalar(as_int(rstd), as_int(t), -1.0, float(0x5F3759DF), ALU.mult, ALU.add))
                for _ in range(3):
                    step(v.tensor_scalar(t, rstd, rstd, var, ALU.mult, ALU.mult))
                    step(v.tensor_scalar(t, t, -0.5, 1.5, ALU.mult, ALU.add))
                    step(v.tensor_scalar(rstd, rstd, t, None, ALU.mult))
                step(v.scalar_tensor_tensor(out=xr, in0=xr, scalar=mean, in1=bgb(1), op0=ALU.subtract, op1=ALU.mult))
                v.scalar_tensor_tensor(out=xr, in0=xr, scalar=rstd, in1=bgb(2), op0=ALU.mult, op1=ALU.add).then_inc(s_ln, 1)

            quads = lambda ap: ap.rearrange("p (d f) -> p d f", f=4)
            pairs = lambda ap: ap.rearrange("p (d f) -> p d f", f=2)

            def rotate_products(s, inner):
                table = lambda k: rot[:, bass.ds(s, 1), k:k + 4].to_broadcast([P, H // 4, 4])
                xr = row(xbuf, s % XB)
                dve.wait_ge(s_ln, s + 1)
                step(v.tensor_tensor(quads(turned[:]), quads(xr), table(4), ALU.mult))
                if inner or s >= 1:
                    dve.wait_ge(s_y, s * 16)
                step(v.tensor_tensor(quads(y[:]), quads(xr), table(0), ALU.mult))

            def rotate_sums():
                step(v.tensor_tensor(pairs(y[:])[:, :, 0], pairs(y[:])[:, :, 0], pairs(turned[:])[:, :, 1], ALU.add))
                v.tensor_tensor(pairs(y[:])[:, :, 1], pairs(y[:])[:, :, 1], pairs(turned[:])[:, :, 0], ALU.add).then_inc(s_done, 1)

            def iteration(s, inner=False):
                chain.clear()
                ahead, here = there(s, 1, inner), there(s, 0, inner)
                back, last = there(s, -1, inner), there(s, -2, inner)
                if here and not inner and s == 0:
                    b, r = 0, 0
                elif here:
                    b, r = slot_value(dve, BUF, s, 1), slot_value(dve, RANK, s, E - 1)
                if last:
                    b2, b3 = slot_value(dve, BUF, s - 2, 1), slot_value(dve, BUF3, s - 2, RB - 1)
                    residual(s - 2, b2, inner)
                if here:
                    dve.wait_ge(s_wi, r + 1)
                    scale_h(s, b, inner)
                if ahead and (inner or s > 0):
                    scale_x(s + 1, inner)
                if back and not here:
                    lo_group(s - 1, 0)
                    lo_group(s - 1, 1)
                if last:
                    normalise(s - 2, b3)
                if back and here:
                    lo_group(s - 1, 0)
                if ahead and not inner and s == 0:
                    lo_x(s + 1)
                if here:
                    z_bank(s, 0, b, inner)
                if last and here:
                    rotate_products(s - 2, inner)
                if back and here:
                    lo_group(s - 1, 1)
                if ahead and (inner or s != 0):
                    lo_x(s + 1)
                if here:
                    z_bank(s, 1, b, inner)
                if last and here:
                    rotate_sums()
                if back:
                    lo_group(s - 1, 2)
                if here:
                    z_bank(s, 2, b, inner)
                if back:
                    lo_group(s - 1, 3)
                if here:
                    z_bank(s, 3, b, inner)
                if last and not here:
                    rotate_products(s - 2, inner)
                    rotate_sums()

            raws = [w[:, 1].rearrange("p a k n -> p (a k n)").bitcast(F32) for w in (wi16, wo16)]
            his = [w[:, 0, 0].rearrange("p k n -> p (k n)") for w in (wi16, wo16)]
            los = [w[:, 0, 1].rearrange("p k n -> p (k n)") for w in (wi16, wo16)]

            def total(m):
                dve.wait_ge(s_bsq, (Q - 1, 2 * Q - 1)[m])
                if m == 0:
                    dve.wait_ge(s_bsqp, 1)
                step(v.reduce_sum(boot_ss[:, 2 * Q + m:2 * Q + m + 1], boot_ss[:, m * Q:(m + 1) * Q], AX.X))
                v.engine_nop().then_inc(s_bsum, 1)

            def lo_parts(m):
                for q in range((Q, WO_SPLIT)[m]):
                    c = slice(q * QN, (q + 1) * QN)
                    dve.wait_ge(s_bhi, m * Q + q + 1)
                    v.scalar_tensor_tensor(out=los[m][:, c], in0=raws[m][:, c], scalar=wscale[:, m:m + 1],
                                           in1=his[m][:, c], op0=ALU.mult, op1=ALU.subtract).then_inc(s_blo, 1)
                dve.wait_ge(s_blo, (Q, Q + WO_SPLIT)[m])

            scale_x(0, False)
            iteration(-1)

            dve.wait_ge(s_angin, 32)
            turns, r = angle[:, 4:6], angle[:, 8:10]
            step(v.tensor_scalar(turns, angle[:, 0:2], 1.0 / 6.283185307179586, TO_INTEGER, ALU.mult, ALU.add))
            step(v.tensor_scalar(turns, turns, -TO_INTEGER, None, ALU.add))
            step(v.tensor_copy(r, angle[:, 0:2]))
            for part in TWO_PI_PARTS:
                step(v.scalar_tensor_tensor(out=r, in0=turns, scalar=-part, in1=r, op0=ALU.mult, op1=ALU.add))
            step(v.tensor_scalar(angle[:, 18:20], r, BELOW_PI, -BELOW_PI, ALU.min, ALU.max))
            step(v.scalar_tensor_tensor(out=r, in0=angle[:, 18:20], scalar=-1.0, in1=angle[:, 18:20],
                                        op0=ALU.mult, op1=ALU.max))
            v.tensor_scalar(angle[:, 16:18], r, -1.0, 1.5707963267948966, ALU.mult, ALU.add).then_inc(s_ang, 1)

            total(0)
            scale_x(1, False)

            dve.wait_ge(s_sin, 1)
            for j in range(4):
                step(v.tensor_copy(spread[:, j * P:(j + 1) * P], angle[:, 20 + j:21 + j].to_broadcast([P, P])))
            v.engine_nop().then_inc(s_onehot, 1)
            lo_parts(0)
            v.engine_nop().then_inc(s_wi, 1)
            dve.wait_ge(s_tabp, 2)
            for col, src, sign in ((0, 0, 1), (1, 0, 1), (2, 1, 1), (3, 1, 1), (4, 2, -1), (5, 2, 1), (6, 3, -1), (7, 3, 1)):
                step(v.tensor_scalar(rot[:, :, col], o_ps[:, src * S:(src + 1) * S], float(sign), None, ALU.mult))
            total(1)
            dve.wait_ge(s_bscale, 2)
            iteration(0)
            lo_parts(1)

            pipeline(dve, iteration)
            v.engine_nop().then_inc(s_res, 1)

        @block.tensor
        def _(pe):
            t = nc.tensor
            fe, first, rank = cols[:, 4:5], cols[:, 2:3], cols[:, 3:4]
            pe.wait_ge(s_less, 1)
            t.matmul(xT_ps[:, 0:1], less, first, start=True, stop=True).then_inc(s_rankp, 1)
            pe.wait_ge(s_onehot, 1)
            t.matmul(xT_ps[0:1, 0:S], iota_f[:, S:S + 1], onehot, start=True, stop=True)
            t.matmul(xT_ps[0:1, S:2 * S], rank, onehot, start=True, stop=True)
            t.matmul(xT_ps[0:1, 2 * S:2 * S + E], fe, onehot_r, start=True, stop=True)
            t.matmul(xT_ps[0:1, 3 * S:3 * S + E + 1], ones, after_r, start=True, stop=True).then_inc(s_tabp, 1)
            pe.wait_ge(s_tables, 2)
            pe.wait_ge(s_ident, 1)

            PASSES = ((1, 0), (0, 1), (0, 0))

            def transpose_h(s, n, inner):
                G = s * NB + n
                pe.wait_ge(s_hs, G + 1)
                if inner or G >= 2:
                    pe.wait_ge(s_hlo, G - 1)
                for c in range(GC):
                    last = t.transpose(hT_ps[:, n % 2, c * P:(c + 1) * P],
                                       hid[:, (n * GC + c) * P:(n * GC + c + 1) * P], ident[:])
                last.then_inc(s_hT, 1)

            def first_product_by_quarters():
                for k in range(KH):
                    pe.wait_ge(s_blo, k + 1)
                    for n in range(NB):
                        cs = slice(n * BANK, (n + 1) * BANK)
                        for a, w in PASSES:
                            last = t.matmul(z_ps[:, n, :], xT16[:, a, k, :], wi16[:, 0, w, k, cs],
                                            start=(k == 0 and (a, w) == PASSES[0]),
                                            stop=(k == KH - 1 and (a, w) == PASSES[-1]))
                        if k == KH - 1:
                            last.then_inc(s_g1, 1)

            def first_product(s, n, b, inner):
                if inner or s >= 1:
                    pe.wait_ge(s_z, (s - 1) * NB + n + 1)
                cs = slice(n * BANK, (n + 1) * BANK)
                for k in range(KH):
                    for a, w in PASSES:
                        last = t.matmul(z_ps[:, n, :], xT16[:, a, k, :], wi16[:, bass.ds(b, 1), w, k, cs],
                                        start=(k == 0 and (a, w) == PASSES[0]),
                                        stop=(k == KH - 1 and (a, w) == PASSES[-1]))
                last.then_inc(s_g1, 1)

            def wait_boot_wo(q):
                if q < WO_SPLIT:
                    pe.wait_ge(s_blo, Q + q + 1)
                else:
                    pe.wait_ge(s_bpool, q - WO_SPLIT + 1)

            def second_product(s, n, b):
                pe.wait_ge(s_hlo, s * NB + n + 1)
                for c in range(GC):
                    for a, w in PASSES:
                        last = t.matmul(o_ps[:], hT16[:, n % 2, a, c, :], wo16[:, bass.ds(b, 1), w, n * GC + c, :],
                                        start=(n == 0 and c == 0 and (a, w) == PASSES[0]),
                                        stop=(n == NB - 1 and c == GC - 1 and (a, w) == PASSES[-1]))
                last.then_inc(s_g2, 1)

            def iteration(s, inner=False):
                if there(s, -2, inner):
                    b2 = slot_value(pe, BUF, s - 2, 1)
                    if not inner and s == 2:
                        wait_boot_wo(NB - 1)
                    second_product(s - 2, NB - 1, b2)
                if there(s, 0, inner):
                    b, r = slot_value(pe, BUF, s, 1), slot_value(pe, RANK, s, E - 1)
                if there(s, 0, inner):
                    pe.wait_ge(s_xlo, s + 1)
                    if not inner and s == 0:
                        first_product_by_quarters()
                    else:
                        pe.wait_ge(s_wi, r + 1)
                        for n in range(NB - 1):
                            first_product(s, n, b, inner)
                if there(s, -1, inner):
                    transpose_h(s - 1, 0, inner)
                if there(s, 0, inner) and (inner or s > 0):
                    first_product(s, NB - 1, b, inner)
                if there(s, -1, inner):
                    transpose_h(s - 1, 1, inner)
                if there(s, 1, inner):
                    pe.wait_ge(s_xs, s + 2)
                    for k in range(KH):
                        last = t.transpose(xT_ps[:, k * P:(k + 1) * P], xs[:, k * P:(k + 1) * P], ident[:])
                    last.then_inc(s_xT, 1)
                if there(s, -1, inner):
                    b1 = slot_value(pe, BUF, s - 1, 1)
                    boot = not inner and s == 1
                    if not boot:
                        pe.wait_ge(s_wo, slot_value(pe, RANK, s - 1, E - 1) + 1)
                        if inner or s >= 2:
                            pe.wait_ge(s_res, s - 1)
                    for n in range(NB - 1):
                        if n:
                            transpose_h(s - 1, n + 1, inner)
                        if boot:
                            wait_boot_wo(n)
                        second_product(s - 1, n, b1)

            iteration(-1)
            pe.wait_ge(s_onehot, 2)
            for j in range(4):
                last = t.matmul(o_ps[:, j * S:(j + 1) * S], spread[:, j * P:(j + 1) * P], onehot, start=True, stop=True)
            last.then_inc(s_tabp, 1)
            iteration(0)
            pipeline(pe, iteration)


_INS = ["x", "itok_B_0_7", "condB_theta", "condB_phi", "L0_cond_Wi", "L0_cond_bi", "L0_cond_Wo",
        "L0_cond_bo", "L0_cond_gamma", "L0_cond_beta"]


def kernel(**inputs):
    import numpy as np
    import concourse.bacc as bacc
    from concourse import mybir as mb
    from concourse.bass_utils import run_bass_kernel_spmd

    nc = bacc.Bacc("TRN2", target_bir_lowering=False, num_devices=1,
                   dynamic_dma_scratch_size=1024)
    arrays, args = {}, []
    for name in _INS:
        a = np.ascontiguousarray(inputs[name])
        arrays[f"in_{name}"] = a
        args.append(nc.dram_tensor(f"in_{name}", a.shape, mb.dt.from_np(a.dtype), kind="ExternalInput").ap())
    shape = arrays["in_x"].shape
    args.append(nc.dram_tensor("out", shape, mb.dt.float32, kind="ExternalOutput").ap())
    expert_mlp_rotate_kernel(nc, *args)
    result = run_bass_kernel_spmd(nc, [arrays], core_ids=[0])
    return result.results[0]["out"]
```
